# Optimizing a Trainium2 kernel written in Bass

```python
import numpy as np
import jax
import jax.numpy as jnp

def _softmax(x, axis=-1):
    return jax.nn.softmax(x, axis=axis)

def _gelu(x):
    return jax.nn.gelu(x, approximate=True)

def _silu(x):
    return jax.nn.silu(x)

def _sigmoid(x):
    return jax.nn.sigmoid(x)

def _layernorm(x, axis=-1, eps=1e-05):
    m = jnp.mean(x, axis=axis, keepdims=True)
    v = jnp.var(x, axis=axis, keepdims=True)
    return (x - m) / jnp.sqrt(v + eps)

def _scatter_add(tgt, idx, src, axis=0):
    return tgt.at[idx].add(src)

def _segment_sum(src, seg, n):
    return jax.ops.segment_sum(src, seg, n)
kernel_name = 'mk_xattn_ffn_d1_seqx_r4_b34ea5'

def setup_inputs(seed: int=0):
    np.random.seed(seed)
    _w = jnp.asarray

    def _rec_inputs():
        import jax
        import jax.numpy as jnp
        _rk = jax.random.key(seed)
        x = -0.0002928 + 1 * jax.random.normal(jax.random.fold_in(_rk, 1), (8, 256, 256), jnp.float32)
        _lenS = 256 - jax.random.randint(jax.random.fold_in(_rk, 7), (8,), 0, max(1, 256 // 4) + 1, jnp.int32)
        _lenS2 = 77 - jax.random.randint(jax.random.fold_in(_rk, 8), (8,), 0, max(1, 77 // 4) + 1, jnp.int32)
        _ctx_1024P = jax.random.normal(jax.random.fold_in(_rk, 11), (8, 16, 256), jnp.float32)
        _ctx_1024c = jax.random.dirichlet(jax.random.fold_in(_rk, 511), 0.3 * jnp.ones((16,), jnp.float32), (8, 77))
        _ctx_1024t = jnp.einsum('bsk,bkd->bsd', _ctx_1024c, _ctx_1024P)
        _ctx_1024t = _ctx_1024t * jax.lax.rsqrt(jnp.mean(jnp.square(_ctx_1024t)) + 1e-12) * 0.953939
        ctx_1024 = 4.13588e-05 + 0.999923 * (_ctx_1024t + 0.3 * jax.random.normal(jax.random.fold_in(_rk, 611), (8, 77, 256), jnp.float32))
        return (x, ctx_1024)
    x, ctx_1024 = _rec_inputs()

    def _L0_xattn_setup():
        import jax, jax.numpy as jnp
        import numpy as np
        DIM = 256
        NUM_HEADS = 16
        DIM_HEAD = 64
        INNER = NUM_HEADS * DIM_HEAD
        SCALE = DIM_HEAD ** (-0.5)

        def _layernorm(x, gamma, beta, eps=1e-05):
            mu = jnp.mean(x, axis=-1, keepdims=True)
            var = jnp.mean(jnp.square(x - mu), axis=-1, keepdims=True)
            return (x - mu) * jax.lax.rsqrt(var + eps) * gamma + beta
        key = jax.random.key(seed)
        ks = jax.random.split(key, 8)
        B, SQ, SK = (2, 512, 1024)
        x = jax.random.normal(ks[0], (B, SQ, DIM), dtype=jnp.float32)
        context = jax.random.normal(ks[1], (B, SK, DIM), dtype=jnp.float32)
        ln_gamma = jnp.ones((DIM,), jnp.float32)
        ln_beta = jnp.zeros((DIM,), jnp.float32)
        w_q = jax.random.normal(ks[2], (DIM, INNER), dtype=jnp.float32) / np.sqrt(DIM)
        w_kv = jax.random.normal(ks[3], (DIM, 2 * INNER), dtype=jnp.float32) / np.sqrt(DIM)
        w_out = jax.random.normal(ks[4], (INNER, DIM), dtype=jnp.float32) / np.sqrt(INNER)
        b_out = jnp.zeros((DIM,), jnp.float32)
        gate = jnp.array([0.5], jnp.float32)
        return {'x': x, 'context': context, 'ln_gamma': ln_gamma, 'ln_beta': ln_beta, 'w_q': w_q, 'w_kv': w_kv, 'w_out': w_out, 'b_out': b_out, 'gate': gate}
    _L0_xattn_all = _L0_xattn_setup()
    _L0_xattn_in = {k: v for k, v in _L0_xattn_all.items() if k in ('ln_gamma', 'ln_beta', 'w_q', 'w_kv', 'w_out', 'b_out', 'gate')}
    del _L0_xattn_all

    def _L0_ffn_setup():
        import jax, jax.numpy as jnp
        import numpy as np
        DIM = 256
        HIDDEN = 768
        SCALE = 1.0 / 127.0

        def _dequant(w_int, dtype):
            return w_int.astype(dtype) * jnp.asarray(SCALE, dtype)
        key = jax.random.key(seed)
        k_x, k_g, k_u, k_d = jax.random.split(key, 4)
        x = jax.random.normal(k_x, (4, 512, DIM), dtype=jnp.float32)
        w_gate = jax.random.randint(k_g, (HIDDEN, DIM), -127, 128, dtype=jnp.int32)
        w_up = jax.random.randint(k_u, (HIDDEN, DIM), -127, 128, dtype=jnp.int32)
        w_down = jax.random.randint(k_d, (DIM, HIDDEN), -127, 128, dtype=jnp.int32)
        return {'x': x, 'w_gate': w_gate, 'w_up': w_up, 'w_down': w_down}
    _L0_ffn_all = _L0_ffn_setup()
    _L0_ffn_in = {k: v for k, v in _L0_ffn_all.items() if k in ('w_gate', 'w_up', 'w_down')}
    del _L0_ffn_all
    return {'x': x, 'ctx_1024': ctx_1024, 'L0_xattn_ln_gamma': _L0_xattn_in['ln_gamma'], 'L0_xattn_ln_beta': _L0_xattn_in['ln_beta'], 'L0_xattn_w_q': _L0_xattn_in['w_q'], 'L0_xattn_w_kv': _L0_xattn_in['w_kv'], 'L0_xattn_w_out': _L0_xattn_in['w_out'], 'L0_xattn_b_out': _L0_xattn_in['b_out'], 'L0_xattn_gate': _L0_xattn_in['gate'], 'L0_ffn_w_gate': _L0_ffn_in['w_gate'], 'L0_ffn_w_up': _L0_ffn_in['w_up'], 'L0_ffn_w_down': _L0_ffn_in['w_down']}

def reference(x, ctx_1024, L0_xattn_ln_gamma, L0_xattn_ln_beta, L0_xattn_w_q, L0_xattn_w_kv, L0_xattn_w_out, L0_xattn_b_out, L0_xattn_gate, L0_ffn_w_gate, L0_ffn_w_up, L0_ffn_w_down):
    import jax
    import jax.numpy as jnp

    def _L0_xattn_ref(x, context, ln_gamma, ln_beta, w_q, w_kv, w_out, b_out, gate):
        import jax, jax.numpy as jnp
        import numpy as np
        DIM = 256
        NUM_HEADS = 16
        DIM_HEAD = 64
        INNER = NUM_HEADS * DIM_HEAD
        SCALE = DIM_HEAD ** (-0.5)

        def _layernorm(x, gamma, beta, eps=1e-05):
            mu = jnp.mean(x, axis=-1, keepdims=True)
            var = jnp.mean(jnp.square(x - mu), axis=-1, keepdims=True)
            return (x - mu) * jax.lax.rsqrt(var + eps) * gamma + beta
        B, SQ, _ = x.shape
        SK = context.shape[1]
        xn = _layernorm(x, ln_gamma, ln_beta)
        q = (xn @ w_q).reshape(B, SQ, NUM_HEADS, DIM_HEAD)
        kv = context @ w_kv
        k, v = jnp.split(kv, 2, axis=-1)
        k = k.reshape(B, SK, NUM_HEADS, DIM_HEAD)
        v = v.reshape(B, SK, NUM_HEADS, DIM_HEAD)
        scores = jnp.einsum('bqhd,bkhd->bhqk', q * SCALE, k)
        attn = jax.nn.softmax(scores, axis=-1)
        out = jnp.einsum('bhqk,bkhd->bqhd', attn, v).reshape(B, SQ, INNER)
        out = out @ w_out + b_out
        return out * jnp.tanh(gate[0])

    def _L0_ffn_ref(x, w_gate, w_up, w_down):
        import jax, jax.numpy as jnp
        import numpy as np
        DIM = 256
        HIDDEN = 768
        SCALE = 1.0 / 127.0

        def _dequant(w_int, dtype):
            return w_int.astype(dtype) * jnp.asarray(SCALE, dtype)
        wg = _dequant(w_gate, x.dtype)
        wu = _dequant(w_up, x.dtype)
        wd = _dequant(w_down, x.dtype)
        gate = jnp.einsum('bsd,hd->bsh', x, wg)
        up = jnp.einsum('bsd,hd->bsh', x, wu)
        h = jax.nn.silu(gate) * up
        return jnp.einsum('bsh,dh->bsd', h, wd)
    x = x + _L0_xattn_ref(_layernorm(x, axis=-1), ctx_1024, L0_xattn_ln_gamma, L0_xattn_ln_beta, L0_xattn_w_q, L0_xattn_w_kv, L0_xattn_w_out, L0_xattn_b_out, L0_xattn_gate)
    x = x + _L0_ffn_ref(_layernorm(x, axis=-1), L0_ffn_w_gate, L0_ffn_w_up, L0_ffn_w_down)
    return x

_drawn_inputs = setup_inputs


def setup_inputs(seed=0):
    import zlib

    import numpy as np

    out = dict(_drawn_inputs(seed))
    spreads = {'L0_xattn_ln_gamma': (1.0, 0.2),
     'L0_xattn_ln_beta': (0.0, 0.539),
     'L0_xattn_b_out': (0.0, 0.1)}
    factors = {}
    for name, (base, spread) in spreads.items():
        noise = np.random.default_rng([zlib.crc32(name.encode()), seed]).standard_normal(out[name].shape)
        drawn = base * np.exp(spread * noise) if base else spread * noise
        out[name] = jnp.asarray(drawn.astype(out[name].dtype))
    for name, factor in factors.items():
        out[name] = (out[name] * factor).astype(out[name].dtype)
    return out
```

```python
from contextlib import ExitStack

import concourse.bass as bass
from concourse import mybir

F32 = mybir.dt.float32
F32R = mybir.dt.float32r
I32 = mybir.dt.int32
ACT = mybir.ActivationFunctionType
ALU = mybir.AluOpType
AXIS_X = mybir.AxisListType.X

P = 128
BANK = 512
HEADS = 16
EPS = 1e-5
RSQRT_SEED = 0x5F3759DF
QUANT = 1.0 / 127.0


def xattn_ffn_kernel(nc, x, ctx_in, ln_gamma, ln_beta, w_q, w_kv, w_out, b_out, gate,
                     w_gate, w_up, w_down, out):
    B, S, D = x.shape
    K = ctx_in.shape[1]
    INNER = w_q.shape[1]
    DH = INNER // HEADS
    HID = w_gate.shape[0]
    DC = D // P
    NT = S // P
    IC = INNER // P
    FC = HID // P
    HK = HEADS * K
    HG = HEADS // 2
    HB = HG // 2
    CR = B * K
    RC = (CR + P - 1) // P
    HALF = B // 2
    SCALE = DH ** -0.5
    assert HB * K <= BANK and DC == 2 and NT == 2

    x_dram = x.rearrange("b (t p) d -> p b t d", p=P)
    out_dram = out.rearrange("b (t p) d -> p b t d", p=P)
    ctx_rows = ctx_in.rearrange("b k d -> (b k) d")
    v_scratch = nc.dram_tensor("v_scratch", (CR, INNER), F32, kind="Internal").ap()

    stack = ExitStack()
    with stack:
        def sem(name):
            return stack.enter_context(nc.semaphore(name))

        def sb(name, shape, dt=F32, where=stack):
            return where.enter_context(nc.sbuf_tensor(name, shape, dt))

        t_all = sb("t_all", [P, DC, B, HK])
        wo_hi = sb("wo_hi", [P, IC, D], F32R)
        wo_lo = sb("wo_lo", [P, IC, D], F32R)
        wg = sb("wg", [P, DC, HID], F32R)
        wu = sb("wu", [P, DC, HID], F32R)
        wd = sb("wd", [P, FC, D], F32R)
        ident = sb("ident", [P, P])
        gamma = sb("gamma", [P, DC])
        beta = sb("beta", [P, DC])
        tgate = sb("tgate", [P, 1])
        bias = sb("bias", [P, D])
        mean1 = sb("mean1", [P, B * NT])
        rstd1 = sb("rstd1", [P, B * NT])

        def rsqrt(dve, step, r, v, tmp):
            step(nc.vector.tensor_single_scalar(tmp.bitcast(I32), v.bitcast(I32), 1, ALU.logical_shift_right))
            step(nc.vector.tensor_scalar(r.bitcast(I32), tmp.bitcast(I32), -1, RSQRT_SEED, ALU.mult, ALU.add))
            for _ in range(3):
                step(nc.vector.tensor_tensor(tmp, r, r, ALU.mult))
                step(nc.vector.scalar_tensor_tensor(tmp, tmp, -0.5, v, ALU.mult, ALU.mult))
                step(nc.vector.scalar_tensor_tensor(r, tmp, 1.5, r, ALU.add, ALU.mult))

        setup(nc, locals())
        attend(nc, locals())


def setup(nc, env):
    (B, K, D, DC, NT, IC, FC, HK, CR, RC, HALF, DH, INNER, HID) = (
        env[n] for n in "B K D DC NT IC FC HK CR RC HALF DH INNER HID".split())
    t_all, wo_hi, wo_lo, wg, wu, wd, ident = (
        env[n] for n in "t_all wo_hi wo_lo wg wu wd ident".split())
    gamma, beta, tgate, bias, mean1, rstd1 = (env[n] for n in "gamma beta tgate bias mean1 rstd1".split())
    NB = 8

    stack = ExitStack()
    with stack:
        def sem(name):
            return stack.enter_context(nc.semaphore(name))

        def sb(name, shape, dt=F32):
            return stack.enter_context(nc.sbuf_tensor(name, shape, dt))

        stage = t_all[:].rearrange("p c b n -> p (c b n)")
        used = [0]

        def staged(*shape):
            n = 1
            for s in shape:
                n *= s
            a = stage[:, used[0]:used[0] + n]
            used[0] += n
            names = "abc"[:len(shape)]
            if len(shape) == 1:
                return a
            return a.rearrange(f"p ({' '.join(names)}) -> p {' '.join(names)}", **dict(zip(names, shape)))

        wk_raw = staged(DC, INNER)
        wv_raw = staged(DC, INNER)
        wq_raw = staged(DC, INNER)
        wo_raw = staged(IC, D)
        ctx_raw = staged(RC, D)
        wg_raw = staged(FC, D)
        wu_raw = staged(FC, D)
        wd_raw = staged(DC, HID)
        v_out = staged(RC, INNER)
        assert used[0] <= DC * B * HK

        wk_hi = sb("wk_hi", [P, DC, INNER], F32R)
        wk_lo = sb("wk_lo", [P, DC, INNER], F32R)
        wv_hi = wo_hi[:].rearrange("p i d -> p (i d)").rearrange("p (c n) -> p c n", c=DC)
        wv_lo = wo_lo[:].rearrange("p i d -> p (i d)").rearrange("p (c n) -> p c n", c=DC)
        wqt_hi = sb("wqt_hi", [P, IC, D], F32R)
        wqt_lo = sb("wqt_lo", [P, IC, D], F32R)
        ct_hi = sb("ct_hi", [P, DC, CR], F32R)
        ct_lo = sb("ct_lo", [P, DC, CR], F32R)
        kt_hi = sb("kt_hi", [P, IC, CR], F32R)
        kt_lo = sb("kt_lo", [P, IC, CR], F32R)
        x_stat = sb("x_stat", [P, 3, NT, D])
        stats = sb("stats", [P, 6])
        mv = sb("mv", [P, B * NT, 2])
        var_eps = sb("var_eps", [P, B * NT])
        r_first = sb("r_first", [P, B * NT])
        tmp = sb("tmp", [P, B * NT])
        ps = stack.enter_context(nc.psum_tensor("ps_setup", [P, NB, BANK], F32))

        jobs = []
        jobs += [("ctx", r) for r in range(RC)]
        jobs += [("v", r, n) for r in range(RC) for n in range(2)]
        jobs += [("k", i, n) for i in range(IC) for n in range(2)]
        jobs += [("wq", i) for i in range(IC)]
        jobs += [("wg", f) for f in range(FC)] + [("wu", f) for f in range(FC)] + [("wd", f) for f in range(FC)]
        first_t = len(jobs)
        jobs += [("t", h, n) for h in range(HEADS) for n in range(2)]
        split = {"ctx", "k", "wq"}
        bank_of, at = [], 0
        for j in jobs:
            if j[0] == "t":
                at += at % 2
                bank_of.append(at % NB)
                at += 2
            else:
                bank_of.append(at % NB)
                at += 1
        by_act, by_dve, a, d = [], [], 0, 0
        for n, j in enumerate(jobs):
            if j[0] in split:
                a, d = a + 1, d + 1
            elif n % 2:
                a += 1
            else:
                d += 1
            by_act.append(a)
            by_dve.append(d)
        last = {j[0]: n for n, j in enumerate(jobs)}
        holder = {}
        before = []
        for n, j in enumerate(jobs):
            banks = [bank_of[n]] + ([bank_of[n] + 1] if j[0] == "t" else [])
            before.append(sorted({holder[k] for k in banks if k in holder}))
            holder.update({k: n for k in banks})

        s_in = {n: sem(f"in_{n}") for n in "ctx wk wv wq wo wg wu wd small".split()}
        s_ident0 = sem("ident_zeroed")
        s_ident = sem("ident_ready")
        s_job = sem("job_done")
        s_act = sem("job_copied_by_act")
        s_dve = sem("job_copied_by_dve")
        s_wkh, s_wkl = sem("wk_hi_ready"), sem("wk_lo_ready")
        s_wvh, s_wvl = sem("wv_hi_ready"), sem("wv_lo_ready")
        s_woh, s_wol = sem("wo_hi_ready"), sem("wo_lo_ready")
        s_float = sem("ints_made_float")
        s_tgate = sem("tanh_gate_ready")
        s_bias = sem("bias_ready")
        s_xs = [sem(f"x_for_stats_{i}") for i in range(3)]
        s_stat = sem("stats_done")
        s_aggr = sem("aggr_done")
        s_ln = sem("norm_scalars_step")
        s_vout = sem("v_stored")

        def evacuated(eng, n):
            j = jobs[n]
            if j[0] in split or n % 2:
                eng.wait_ge(s_act, by_act[n])
            if j[0] in split or not n % 2:
                eng.wait_ge(s_dve, by_dve[n])

        def rows(r):
            return min(P, CR - r * P)

        def psum_of(n):
            j, b = jobs[n], bank_of[n]
            if j[0] == "ctx":
                return ps[:, b, 0:DC * P].rearrange("p (c r) -> p c r", c=DC)[:, :, 0:rows(j[1])]
            if j[0] == "v":
                return ps[0:rows(j[1]), b, :]
            if j[0] == "k":
                return ps[:, b, 0:HALF * K]
            if j[0] in ("wg", "wu"):
                return ps[:, b, 0:DC * P].rearrange("p (c r) -> p c r", c=DC)
            if j[0] in ("wq", "wd"):
                return ps[:, b, 0:D]
            return ps[:, b:b + 2, 0:HALF * K].rearrange("p c (b k) -> p c b k", k=K)

        def target(n):
            j = jobs[n]
            if j[0] == "ctx":
                cols = slice(j[1] * P, j[1] * P + rows(j[1]))
                return ct_hi[:, :, cols], ct_lo[:, :, cols]
            if j[0] == "v":
                return (v_out[0:rows(j[1]), j[1], j[2] * BANK:(j[2] + 1) * BANK],)
            if j[0] == "k":
                cols = slice(j[2] * HALF * K, (j[2] + 1) * HALF * K)
                return kt_hi[:, j[1], cols], kt_lo[:, j[1], cols]
            if j[0] == "wq":
                return wqt_hi[:, j[1], :], wqt_lo[:, j[1], :]
            if j[0] in ("wg", "wu"):
                w = wg if j[0] == "wg" else wu
                return (w[:, :, j[1] * P:(j[1] + 1) * P],)
            if j[0] == "wd":
                return (wd[:, j[1], :],)
            return (t_all[:, :, j[2] * HALF:(j[2] + 1) * HALF, j[1] * K:(j[1] + 1) * K],)

        block = stack.enter_context(nc.Block())

        @block.sync
        def _(sp):
            x_dram = env["x_dram"]
            sp.dma_start(ctx_raw[:, 0:RC - 1, :],
                         env["ctx_rows"][0:(RC - 1) * P, :].rearrange("(r p) d -> p r d", p=P)).then_inc(s_in["ctx"], 16)
            sp.dma_start(ctx_raw[0:rows(RC - 1), RC - 1, :],
                         env["ctx_rows"][(RC - 1) * P:CR, :]).then_inc(s_in["ctx"], 16)
            w_kv = env["w_kv"].rearrange("(c p) n -> p c n", p=P)
            sp.dma_start(wv_raw, w_kv[:, :, INNER:2 * INNER]).then_inc(s_in["wv"], 16)
            sp.dma_start(wk_raw, w_kv[:, :, 0:INNER]).then_inc(s_in["wk"], 16)
            sp.dma_start(wq_raw, env["w_q"].rearrange("(c p) n -> p c n", p=P)).then_inc(s_in["wq"], 16)
            for name, raw, w in (("wg", wg_raw, env["w_gate"]), ("wu", wu_raw, env["w_up"]),
                                 ("wd", wd_raw, env["w_down"])):
                sp.dma_start(raw.bitcast(I32), w.rearrange("(r p) n -> p r n", p=P)).then_inc(s_in[name], 16)
            sp.dma_start(wo_raw, env["w_out"].rearrange("(i p) n -> p i n", p=P)).then_inc(s_in["wo"], 16)
            for b in range(B):
                if b >= 3:
                    sp.wait_ge(s_stat, NT * (b - 2))
                sp.dma_start(x_stat[:, b % 3], x_dram[:, b]).then_inc(s_xs[b % 3], 16)
            for r in range(RC):
                for n in range(2):
                    evacuated(sp, jobs.index(("v", r, n)))
                sp.dma_start(env["v_scratch"][r * P:r * P + rows(r), :], v_out[0:rows(r), r, :]).then_inc(s_vout, 16)
            sp.wait_ge(s_vout, 16 * RC)

        @block.gpsimd
        def _(pool):
            nc.gpsimd.memset(ident[:], 0.0).then_inc(s_ident0, 1)
            pool.wait_ge(s_ident0, 1)
            nc.gpsimd.affine_select(out=ident[:], in_=ident[:], compare_op=ALU.not_equal, fill=1.0,
                                    base=0, pattern=[[-1, P]], channel_multiplier=1).then_inc(s_ident, 1)
            pool.wait_ge(s_in["wk"], 16)
            pool.wait_ge(s_wkh, 1)
            nc.gpsimd.tensor_tensor(wk_lo[:], wk_raw, wk_hi[:].bitcast(F32), ALU.subtract).then_inc(s_wkl, 1)
            pool.wait_ge(s_in["wo"], 16)
            pool.wait_ge(s_woh, 1)
            nc.gpsimd.tensor_tensor(wo_lo[:], wo_raw, wo_hi[:].bitcast(F32), ALU.subtract).then_inc(s_wol, 1)

        @block.scalar
        def _(act):
            act.dma_start(gamma[:], env["ln_gamma"].rearrange("(c p) -> p c", p=P),
                          allow_slow_non_contiguous=True).then_inc(s_in["small"], 16)
            act.dma_start(beta[:], env["ln_beta"].rearrange("(c p) -> p c", p=P),
                          allow_slow_non_contiguous=True).then_inc(s_in["small"], 16)
            act.dma_start(tgate[:], env["gate"].rearrange("(a n) -> a n", a=1).to_broadcast([P, 1])).then_inc(s_in["small"], 16)
            act.dma_start(bias[:], env["b_out"].rearrange("(a n) -> a n", a=1).to_broadcast([P, D])).then_inc(s_in["small"], 16)
            act.wait_ge(s_in["small"], 64)
            nc.scalar.activation(tgate[:], tgate[:], ACT.Tanh).then_inc(s_tgate, 1)

            def copy(n):
                act.wait_ge(s_job, n + 1)
                if n in (first_t, first_t + 1):
                    act.wait_ge(s_vout, 16 * RC)
                    act.wait_ge(s_wol, 1)
                nc.scalar.copy(target(n)[0], psum_of(n)).then_inc(s_act, 1)

            mine = [n for n, j in enumerate(jobs) if j[0] in split or n % 2]
            for n in mine:
                if jobs[n] == ("k", 0, 0):
                    pass
                copy(n)
                if jobs[n] == ("ctx", RC - 1):
                    act.wait_ge(s_in["wk"], 16)
                    nc.scalar.copy(wk_hi[:], wk_raw).then_inc(s_wkh, 1)
                if jobs[n] == ("k", IC - 1, 1):
                    act.wait_ge(s_in["wo"], 16)
                    act.wait_ge(s_job, last["v"] + 1)
                    nc.scalar.copy(wo_hi[:], wo_raw).then_inc(s_woh, 1)

        @block.vector
        def _(dve):
            steps = [0]

            def step(ins):
                steps[0] += 1
                ins.then_inc(s_ln, 1)
                dve.wait_ge(s_ln, steps[0])

            def copy(n):
                dve.wait_ge(s_job, n + 1)
                if jobs[n][0] in split:
                    hi, lo = target(n)
                    dve.wait_ge(s_act, by_act[n])
                    nc.vector.tensor_tensor(lo, psum_of(n), hi.bitcast(F32), ALU.subtract).then_inc(s_dve, 1)
                else:
                    if n in (first_t, first_t + 1):
                        dve.wait_ge(s_vout, 16 * RC)
                        dve.wait_ge(s_wol, 1)
                    nc.vector.tensor_copy(target(n)[0], psum_of(n)).then_inc(s_dve, 1)

            def stat(i):
                b, t = divmod(i, NT)
                dve.wait_ge(s_xs[b % 3], 16 * (b // 3 + 1))
                if i:
                    dve.wait_ge(s_aggr, i)
                nc.vector.bn_stats(stats[:], x_stat[:, b % 3, t, :]).then_inc(s_stat, 1)
                dve.wait_ge(s_stat, i + 1)
                nc.vector.bn_aggr(mv[:, i, :], stats[:]).then_inc(s_aggr, 1)

            mine = [n for n, j in enumerate(jobs) if j[0] in split or not n % 2]
            dve.wait_ge(s_in["wv"], 16)
            nc.vector.tensor_copy(wv_hi, wv_raw).then_inc(s_wvh, 1)
            dve.wait_ge(s_wvh, 1)
            nc.vector.tensor_tensor(wv_lo, wv_raw, wv_hi.bitcast(F32), ALU.subtract).then_inc(s_wvl, 1)
            stats_at = 0
            for n in mine:
                copy(n)
                if jobs[n][0] == "v" and jobs[n][1:] == (RC - 1, 0) or jobs[n] == ("k", 0, 0) and s_float is None:
                    pass
                if jobs[n][0] == "k" and stats_at < B * NT:
                    stat(stats_at)
                    stats_at += 1
                if jobs[n] == ("k", 2, 1):
                    for name, raw in (("wg", wg_raw), ("wu", wu_raw), ("wd", wd_raw)):
                        dve.wait_ge(s_in[name], 16)
                        nc.vector.tensor_copy(raw, raw.bitcast(I32)).then_inc(s_float, 1)
                if jobs[n] == ("k", IC - 1, 1):
                    dve.wait_ge(s_tgate, 1)
                    nc.vector.tensor_scalar(bias[:], bias[:], tgate[:, 0:1], None, ALU.mult).then_inc(s_bias, 1)
                    dve.wait_ge(s_aggr, B * NT)
                    var = mv[:, :, 1]
                    step(nc.vector.tensor_copy(mean1[:], mv[:, :, 0]))
                    step(nc.vector.tensor_scalar(var_eps[:], var, EPS, None, ALU.add))
                    env["rsqrt"](dve, step, r_first[:], var_eps[:], tmp[:])
                    step(nc.vector.tensor_tensor(var_eps[:], r_first[:], r_first[:], ALU.mult))
                    step(nc.vector.tensor_tensor(var_eps[:], var_eps[:], var, ALU.mult))
                    step(nc.vector.tensor_scalar(var_eps[:], var_eps[:], EPS, None, ALU.add))
                    env["rsqrt"](dve, step, rstd1[:], var_eps[:], tmp[:])
                    step(nc.vector.tensor_tensor(rstd1[:], rstd1[:], r_first[:], ALU.mult))

        @block.tensor
        def _(pe):
            pe.wait_ge(s_ident, 1)
            pe.wait_ge(s_in["ctx"], 32)
            mm = nc.tensor.matmul
            for n, j in enumerate(jobs):
                kind = j[0]
                for m in before[n]:
                    evacuated(pe, m)
                o = psum_of(n)
                if kind == "ctx":
                    m = rows(j[1])
                    for c in range(DC):
                        ins = nc.tensor.transpose(o[:, c, :], ctx_raw[0:m, j[1], c * P:(c + 1) * P], ident[0:m, 0:m])
                if kind == "v":
                    if j[1:] == (0, 0):
                        evacuated(pe, last["ctx"])
                        pe.wait_ge(s_wvl, 1)
                    cols = slice(j[2] * BANK, (j[2] + 1) * BANK)
                    rs = slice(j[1] * P, j[1] * P + rows(j[1]))
                    for c in range(DC):
                        mm(o, ct_hi[:, c, rs], wv_hi[:, c, cols], start=c == 0, stop=False)
                        mm(o, ct_hi[:, c, rs], wv_lo[:, c, cols], start=False, stop=False)
                        ins = mm(o, ct_lo[:, c, rs], wv_hi[:, c, cols], start=False, stop=c == DC - 1)
                if kind == "k":
                    if j[1:] == (0, 0):
                        pe.wait_ge(s_wkl, 1)
                    cols = slice(j[2] * HALF * K, (j[2] + 1) * HALF * K)
                    ws = slice(j[1] * P, (j[1] + 1) * P)
                    for c in range(DC):
                        mm(o, wk_hi[:, c, ws], ct_hi[:, c, cols], start=c == 0, stop=False)
                        mm(o, wk_hi[:, c, ws], ct_lo[:, c, cols], start=False, stop=False)
                        ins = mm(o, wk_lo[:, c, ws], ct_hi[:, c, cols], start=False, stop=c == DC - 1)
                if kind == "wq":
                    if j[1] == 0:
                        pe.wait_ge(s_in["wq"], 16)
                    for c in range(DC):
                        ins = nc.tensor.transpose(o[:, c * P:(c + 1) * P], wq_raw[:, c, j[1] * P:(j[1] + 1) * P], ident[:])
                if kind in ("wg", "wu"):
                    if j[1] == 0:
                        pe.wait_ge(s_float, 1 if kind == "wg" else 2)
                    raw = wg_raw if kind == "wg" else wu_raw
                    for c in range(DC):
                        ins = nc.tensor.transpose(o[:, c, :], raw[:, j[1], c * P:(c + 1) * P], ident[:])
                if kind == "wd":
                    if j[1] == 0:
                        pe.wait_ge(s_float, 3)
                    for c in range(DC):
                        ins = nc.tensor.transpose(o[:, c * P:(c + 1) * P], wd_raw[:, c, j[1] * P:(j[1] + 1) * P], ident[:])
                if kind == "t":
                    if j[1:] == (0, 0):
                        evacuated(pe, last["k"])
                        evacuated(pe, last["wq"])
                    h, half = j[1:]
                    i, ds = h // 2, slice((h % 2) * DH, (h % 2 + 1) * DH)
                    cols = slice(half * HALF * K, (half + 1) * HALF * K)
                    for c in range(DC):
                        oc = ps[:, bank_of[n] + c, 0:HALF * K]
                        ws = slice(c * P, (c + 1) * P)
                        mm(oc, wqt_hi[ds, i, ws], kt_hi[ds, i, cols], start=True, stop=False)
                        mm(oc, wqt_hi[ds, i, ws], kt_lo[ds, i, cols], start=False, stop=False)
                        ins = mm(oc, wqt_lo[ds, i, ws], kt_hi[ds, i, cols], start=False, stop=True)
                ins.then_inc(s_job, 1)


def attend(nc, env):
    (B, K, D, DC, NT, IC, FC, HK, HG, HB, DH, INNER, SCALE) = (
        env[n] for n in "B K D DC NT IC FC HK HG HB DH INNER SCALE".split())
    t_all, wo_hi, wo_lo, wg, wu, wd, ident = (
        env[n] for n in "t_all wo_hi wo_lo wg wu wd ident".split())
    gamma, beta, tgate, bias, mean1, rstd1 = (env[n] for n in "gamma beta tgate bias mean1 rstd1".split())
    x_dram, out_dram, v_scratch = env["x_dram"], env["out_dram"], env["v_scratch"]
    NU = 2 * NT
    GK = HG * K
    BK = HB * K
    Q = NT * P

    stack = ExitStack()
    with stack:
        def sem(name):
            return stack.enter_context(nc.semaphore(name))

        def sb(name, shape, dt=F32):
            return stack.enter_context(nc.sbuf_tensor(name, shape, dt))

        t_hi = sb("t_hi", [P, DC, HK], F32R)
        t_lo = sb("t_lo", [P, DC, HK], F32R)
        x_ln = sb("x_ln", [P, NT, D])
        x_hat = sb("x_hat", [P, NT, D])
        xn = sb("xn", [P, DC, Q])
        xn_hi = sb("xn_hi", [P, DC, Q], F32R)
        xn_lo = sb("xn_lo", [P, DC, Q], F32R)
        probs = sb("probs", [P, NU, GK])
        top = sb("top", [P, NU, HG])
        total = sb("total", [P, NU, HG])
        pt = sb("pt", [K, HG, Q])
        v = sb("v", [K, INNER])
        o_hi = sb("o_hi", [P, IC, Q], F32R)
        o_lo = sb("o_lo", [P, IC, Q], F32R)
        x_res = sb("x_res", [P, NT, D])
        x1 = sb("x1", [P, NT, D])
        x1_hat = sb("x1_hat", [P, NT, D])
        x2_hi = sb("x2_hi", [P, DC, Q], F32R)
        x2_lo = sb("x2_lo", [P, DC, Q], F32R)
        tanh_g = sb("tanh_g", [P, 2, Q])
        hid = sb("hid", [P, 2, Q])
        h_hi = sb("h_hi", [P, FC, Q], F32R)
        h_lo = sb("h_lo", [P, FC, Q], F32R)
        stats = sb("stats2", [P, NT, 6])
        mv = sb("mv2", [P, NT, 2])
        var_eps = sb("var_eps2", [P, NT])
        rstd = sb("rstd2", [P, NT])
        tmp = sb("tmp2", [P, NT])

        ps_s = stack.enter_context(nc.psum_tensor("ps_s", [P, 2, 2, BANK], F32))
        ps_p = stack.enter_context(nc.psum_tensor("ps_p", [P, 2, BANK], F32))
        ps_m = stack.enter_context(nc.psum_tensor("ps_m", [P, 2, BANK], F32))

        xln_in, xres_in, v_in, y_out = sem("xln_in"), sem("xres_in"), sem("v_in"), sem("y_out")
        scores_done, pt_done, pv_done = sem("scores_done"), sem("pt_done"), sem("pv_done")
        xt_done, x2t_done, gu_done = sem("xt_done"), sem("x2t_done"), sem("gu_done")
        down_done, proj_done = sem("down_done"), sem("proj_done")
        max_done, sub_done, sum_done, rec_done = sem("max_done"), sem("sub_done"), sem("sum_done"), sem("rec_done")
        olo_done, x2lo_done, gated, hid_done = sem("olo_done"), sem("x2lo_done"), sem("gated"), sem("hid_done")
        x1_done, stat_done, ln_step, x1hat_done = sem("x1_done"), sem("stat_done"), sem("ln_step"), sem("x1hat_done")
        rstd_cleared = sem("rstd_cleared")
        xhat_done, y_done = sem("xhat_done"), sem("y_done")
        exp_done, pt_copied, ohi_done = sem("exp_done"), sem("pt_copied"), sem("ohi_done")
        thi_done, tanh_done, hhi_done = sem("thi_done"), sem("tanh_done"), sem("hhi_done")
        x2hi_done, xn_done, xnhi_done = sem("x2hi_done"), sem("xn_done"), sem("xnhi_done")
        probs_done, tlo_done, hlo_done = sem("probs_done"), sem("tlo_done"), sem("hlo_done")
        xres_biased, xnlo_done = sem("xres_biased"), sem("xnlo_done")

        LN_STEPS = 2 + 11

        def batches(eng, body):
            body(0, ffn=False)
            with eng.Fori(1, B - 1) as b:
                body(b)
            body(B - 1, more=False)
            body(B, attn=False, more=False)

        def wait(eng, s, value):
            if isinstance(value, int) and value <= 0:
                return
            eng.wait_ge(s, value)

        block = stack.enter_context(nc.Block())

        @block.sync
        def _(sp):
            sp.dma_start(x_ln[:], x_dram[:, 0]).then_inc(xln_in, 16)
            sp.dma_start(v[:], v_scratch[0:K, :]).then_inc(v_in, 16)

            def body(b, attn=True, ffn=True, more=True):
                if attn:
                    wait(sp, x1_done, NT * b)
                    sp.dma_start(x_res[:], x_dram[:, b]).then_inc(xres_in, 16)
                if more:
                    sp.wait_ge(xhat_done, NT * (b + 1))
                    sp.dma_start(x_ln[:], x_dram[:, b + 1]).then_inc(xln_in, 16)
                if ffn:
                    sp.wait_ge(y_done, NT * b)
                    sp.dma_start(out_dram[:, b - 1], x1[:]).then_inc(y_out, 16)
                if more:
                    sp.wait_ge(pv_done, NU * (b + 1))
                    rows = v_scratch.rearrange("(b k) n -> b k n", k=K)
                    sp.dma_start(v[:], rows[b + 1]).then_inc(v_in, 16)

            batches(sp, body)
            sp.wait_ge(y_out, 16 * B)

        @block.tensor
        def _(pe):
            mm = nc.tensor.matmul

            def scores(b, u):
                g, t = divmod(u, NT)
                if u == 0:
                    pe.wait_ge(xnhi_done, b + 1)
                    pe.wait_ge(xnlo_done, b + 1)
                    pe.wait_ge(thi_done, b + 1)
                    pe.wait_ge(tlo_done, b + 1)
                wait(pe, sub_done, NU * b + u - 1)
                qs = slice(t * P, (t + 1) * P)
                for r in range(2):
                    o = ps_s[:, u % 2, r, 0:BK]
                    cols = slice((g * HG + r * HB) * K, (g * HG + (r + 1) * HB) * K)
                    for c in range(DC):
                        mm(o, xn_hi[:, c, qs], t_hi[:, c, cols], start=c == 0, stop=False)
                        mm(o, xn_hi[:, c, qs], t_lo[:, c, cols], start=False, stop=False)
                        ins = mm(o, xn_lo[:, c, qs], t_hi[:, c, cols], start=False, stop=c == DC - 1)
                ins.then_inc(scores_done, 1)

            def transpose_probs(b, g, t):
                u = NT * g + t
                pe.wait_ge(probs_done, NU * b + u + 1)
                for q in range(2):
                    m = 2 * t + q
                    if m < 2:
                        wait(pe, olo_done, NU * b + 2 * g + m - 1)
                    else:
                        pe.wait_ge(pt_copied, 8 * b + 4 * g + m - 1)
                    for h in range(HB):
                        hh = q * HB + h
                        ins = nc.tensor.transpose(ps_p[0:K, m % 2, h * P:(h + 1) * P],
                                                  probs[:, u, hh * K:(hh + 1) * K], ident[:])
                    ins.then_inc(pt_done, 1)

            def values(b, g):
                pe.wait_ge(pt_copied, 8 * b + 4 * g + 4)
                if g == 0:
                    pe.wait_ge(v_in, 16 * (b + 1))
                for i in range(2):
                    for pair in range(2):
                        for e in range(2):
                            h = 4 * i + 2 * pair + e
                            gh = g * HG + h
                            ins = mm(ps_p[e * DH:(e + 1) * DH, i, pair * Q:(pair + 1) * Q],
                                     v[:, gh * DH:(gh + 1) * DH], pt[:, h, :], start=True, stop=True)
                    ins.then_inc(pv_done, 1)

            def transpose_x(n):
                pe.wait_ge(xhat_done, NT * (n + 1))
                for c in range(DC):
                    for t in range(NT):
                        ins = nc.tensor.transpose(ps_m[:, 1, c * Q + t * P:c * Q + (t + 1) * P],
                                                  x_hat[:, t, c * P:(c + 1) * P], ident[:])
                ins.then_inc(xt_done, 1)

            def transpose_x1(b):
                pe.wait_ge(x1hat_done, NT * b)
                for c in range(DC):
                    for t in range(NT):
                        ins = nc.tensor.transpose(ps_m[:, 0, c * Q + t * P:c * Q + (t + 1) * P],
                                                  x1_hat[:, t, c * P:(c + 1) * P], ident[:])
                ins.then_inc(x2t_done, 1)

            def gate_up(b, f):
                if f == 0:
                    pe.wait_ge(x2hi_done, b)
                    pe.wait_ge(x2lo_done, b)
                if f >= 2:
                    pe.wait_ge(hid_done, FC * (b - 1) + f - 1)
                fs = slice(f * P, (f + 1) * P)
                for w, at in ((wg, 0), (wu, Q)):
                    o = ps_m[:, (f + 1) % 2, at:at + Q]
                    for c in range(DC):
                        mm(o, w[:, c, fs], x2_hi[:, c, :], start=c == 0, stop=False)
                        ins = mm(o, w[:, c, fs], x2_lo[:, c, :], start=False, stop=c == DC - 1)
                ins.then_inc(gu_done, 1)

            def down(b, t):
                if t == 0:
                    pe.wait_ge(hhi_done, FC * b)
                    pe.wait_ge(hlo_done, FC * b)
                o = ps_m[:, (t + 1) % 2, 0:D]
                ts = slice(t * P, (t + 1) * P)
                for f in range(FC):
                    mm(o, h_hi[:, f, ts], wd[:, f, :], start=f == 0, stop=False)
                    ins = mm(o, h_lo[:, f, ts], wd[:, f, :], start=False, stop=f == FC - 1)
                ins.then_inc(down_done, 1)

            def project(b, t):
                if t == 0:
                    pe.wait_ge(ohi_done, NU * (b + 1))
                    pe.wait_ge(olo_done, NU * (b + 1))
                o = ps_m[:, t, 0:D]
                ts = slice(t * P, (t + 1) * P)
                for i in range(IC):
                    mm(o, o_hi[:, i, ts], wo_hi[:, i, :], start=i == 0, stop=False)
                    mm(o, o_hi[:, i, ts], wo_lo[:, i, :], start=False, stop=False)
                    ins = mm(o, o_lo[:, i, ts], wo_hi[:, i, :], start=False, stop=i == IC - 1)
                ins.then_inc(proj_done, 1)

            transpose_x(0)

            def body(b, attn=True, ffn=True, more=True):
                if attn:
                    scores(b, 0)
                    scores(b, 1)
                if ffn:
                    transpose_x1(b)
                    gate_up(b, 0)
                if attn:
                    scores(b, 2)
                if ffn:
                    gate_up(b, 1)
                if attn:
                    transpose_probs(b, 0, 0)
                if ffn:
                    gate_up(b, 2)
                if attn:
                    scores(b, 3)
                if ffn:
                    gate_up(b, 3)
                if attn:
                    transpose_probs(b, 0, 1)
                if ffn:
                    gate_up(b, 4)
                if attn:
                    values(b, 0)
                if ffn:
                    gate_up(b, 5)
                if attn:
                    transpose_probs(b, 1, 0)
                if ffn:
                    down(b, 0)
                if attn:
                    transpose_probs(b, 1, 1)
                if ffn:
                    down(b, 1)
                if attn:
                    values(b, 1)
                if more:
                    wait(pe, y_done, NT * (b - 1) + 1)
                    transpose_x(b + 1)
                if attn:
                    wait(pe, y_done, NT * b)
                    project(b, 0)
                    if more:
                        pe.wait_ge(xn_done, DC * (b + 2))
                    project(b, 1)

            batches(pe, body)

        @block.scalar
        def _(act):
            def exponentials(b, u):
                act.wait_ge(sub_done, NU * b + u + 1)
                nc.scalar.activation(probs[:, u, :], probs[:, u, :], ACT.Exp, scale=SCALE).then_inc(exp_done, 1)

            def copy_pt(b, g, t):
                for q in range(2):
                    m = 4 * g + 2 * t + q
                    act.wait_ge(pt_done, 8 * b + m + 1)
                    if t == 0 and q == 0:
                        wait(act, pv_done, NU * b + 2 * g)
                    nc.scalar.copy(pt[:, q * HB:(q + 1) * HB, t * P:(t + 1) * P],
                                   ps_p[0:K, m % 2, :].rearrange("k (h q) -> k h q", h=HB)).then_inc(pt_copied, 1)

            def copy_o(b, g):
                for i in range(2):
                    n = 2 * g + i
                    act.wait_ge(pv_done, NU * b + n + 1)
                    if n == 0:
                        wait(act, proj_done, NT * b)
                    nc.scalar.copy(o_hi[:, 2 * n:2 * n + 2, :],
                                   ps_p[:, i, :].rearrange("p (i q) -> p i q", i=2)).then_inc(ohi_done, 1)

            def split_t(n):
                if not (isinstance(n, int) and n == 0):
                    act.wait_ge(scores_done, NU * n)
                    act.wait_ge(tlo_done, n)
                nc.scalar.copy(t_hi[:], t_all[:, :, n, :]).then_inc(thi_done, 1)

            def affine_x(n):
                act.wait_ge(xt_done, n + 1)
                if not (isinstance(n, int) and n == 0):
                    act.wait_ge(xnhi_done, n)
                    act.wait_ge(xnlo_done, n)
                for c in range(DC):
                    nc.scalar.activation(xn[:, c, :], ps_m[:, 1, c * Q:(c + 1) * Q], ACT.Identity,
                                         scale=gamma[:, c:c + 1], bias=beta[:, c:c + 1]).then_inc(xn_done, 1)
                act.wait_ge(xn_done, DC * (n + 1))
                if not (isinstance(n, int) and n == 0):
                    act.wait_ge(scores_done, NU * n)
                nc.scalar.copy(xn_hi[:], xn[:]).then_inc(xnhi_done, 1)

            def split_x2(b):
                act.wait_ge(x2t_done, b)
                nc.scalar.copy(x2_hi[:], ps_m[:, 0, :].rearrange("p (c q) -> p c q", c=DC)).then_inc(x2hi_done, 1)

            def tanh(b, f):
                act.wait_ge(gu_done, FC * (b - 1) + f + 1)
                if f >= 2:
                    act.wait_ge(gated, FC * (b - 1) + f - 1)
                nc.scalar.activation(tanh_g[:, f % 2, :], ps_m[:, (f + 1) % 2, 0:Q], ACT.Tanh,
                                     scale=QUANT / 2).then_inc(tanh_done, 1)

            def split_h(b, f):
                act.wait_ge(hid_done, FC * (b - 1) + f + 1)
                nc.scalar.copy(h_hi[:, f, :], hid[:, f % 2, :]).then_inc(hhi_done, 1)

            split_t(0)
            affine_x(0)

            def body(b, attn=True, ffn=True, more=True):
                if attn:
                    exponentials(b, 0)
                if ffn:
                    split_x2(b)
                if attn:
                    exponentials(b, 1)
                if ffn:
                    tanh(b, 0)
                    split_h(b, 0)
                if attn:
                    exponentials(b, 2)
                if ffn:
                    tanh(b, 1)
                if attn:
                    copy_pt(b, 0, 0)
                if ffn:
                    split_h(b, 1)
                    tanh(b, 2)
                if attn:
                    exponentials(b, 3)
                if ffn:
                    split_h(b, 2)
                    tanh(b, 3)
                if attn:
                    copy_pt(b, 0, 1)
                if ffn:
                    split_h(b, 3)
                    tanh(b, 4)
                if more:
                    split_t(b + 1)
                if attn:
                    copy_o(b, 0)
                if ffn:
                    split_h(b, 4)
                    tanh(b, 5)
                    split_h(b, 5)
                if attn:
                    copy_pt(b, 1, 0)
                    copy_pt(b, 1, 1)
                    copy_o(b, 1)
                if more:
                    affine_x(b + 1)

            batches(act, body)

        @block.gpsimd
        def _(pool):
            def normalise(b, u):
                pool.wait_ge(rec_done, NU * b + u + 1)
                p = probs[:, u, :].rearrange("p (h k) -> p h k", k=K)
                nc.gpsimd.tensor_tensor(p, p, total[:, u, :].unsqueeze(2).to_broadcast([P, HG, K]),
                                        ALU.mult).then_inc(probs_done, 1)

            def split_t(n):
                pool.wait_ge(thi_done, n + 1)
                nc.gpsimd.tensor_tensor(t_lo[:], t_all[:, :, n, :], t_hi[:].bitcast(F32),
                                        ALU.subtract).then_inc(tlo_done, 1)

            def split_xn(n):
                pool.wait_ge(xnhi_done, n + 1)
                nc.gpsimd.tensor_tensor(xn_lo[:], xn[:], xn_hi[:].bitcast(F32), ALU.subtract).then_inc(xnlo_done, 1)

            def split_h(b, f):
                pool.wait_ge(hhi_done, FC * (b - 1) + f + 1)
                nc.gpsimd.tensor_tensor(h_lo[:, f, :], hid[:, f % 2, :], h_hi[:, f, :].bitcast(F32),
                                        ALU.subtract).then_inc(hlo_done, 1)

            def bias_x(b):
                pool.wait_ge(xres_in, 16 * (b + 1))
                nc.gpsimd.tensor_tensor(x_res[:], x_res[:], bias[:].unsqueeze(1).to_broadcast([P, NT, D]),
                                        ALU.add).then_inc(xres_biased, 1)

            split_t(0)
            split_xn(0)

            def body(b, attn=True, ffn=True, more=True):
                if attn:
                    normalise(b, 0)
                    normalise(b, 1)
                if ffn:
                    split_h(b, 0)
                if attn:
                    normalise(b, 2)
                if ffn:
                    split_h(b, 1)
                    split_h(b, 2)
                if attn:
                    normalise(b, 3)
                if ffn:
                    split_h(b, 3)
                    split_h(b, 4)
                    split_h(b, 5)
                if more:
                    split_t(b + 1)
                if attn:
                    bias_x(b)
                if more:
                    split_xn(b + 1)

            batches(pool, body)

        @block.vector
        def _(dve):
            def maxima(b, u):
                dve.wait_ge(scores_done, NU * b + u + 1)
                s = ps_s[:, u % 2, :, 0:BK].rearrange("p r (h k) -> p r h k", k=K)
                wait(dve, sub_done, NU * (b - 1) + u + 1)
                nc.vector.reduce_max(top[:, u, :].rearrange("p (r h) -> p r h", r=2), s, AXIS_X).then_inc(max_done, 1)
                dve.wait_ge(max_done, NU * b + u + 1)
                wait(dve, pt_done, 8 * (b - 1) + 2 * (u + 1))
                nc.vector.tensor_tensor(
                    probs[:, u, :].rearrange("p (r h k) -> p r h k", r=2, k=K), s,
                    top[:, u, :].rearrange("p (r h) -> p r h", r=2).unsqueeze(3).to_broadcast([P, 2, HB, K]),
                    ALU.subtract).then_inc(sub_done, 1)

            def sums(b, u):
                dve.wait_ge(exp_done, NU * b + u + 1)
                wait(dve, probs_done, NU * (b - 1) + u + 1)
                nc.vector.reduce_sum(total[:, u, :], probs[:, u, :].rearrange("p (h k) -> p h k", k=K),
                                     AXIS_X).then_inc(sum_done, 1)
                dve.wait_ge(sum_done, NU * b + u + 1)
                nc.vector.reciprocal(total[:, u, :], total[:, u, :]).then_inc(rec_done, 1)

            def split_o(b, g):
                for i in range(2):
                    n = 2 * g + i
                    dve.wait_ge(ohi_done, NU * b + n + 1)
                    if n == 0:
                        wait(dve, proj_done, NT * b)
                    nc.vector.tensor_tensor(o_lo[:, 2 * n:2 * n + 2, :],
                                            ps_p[:, i, :].rearrange("p (i q) -> p i q", i=2),
                                            o_hi[:, 2 * n:2 * n + 2, :].bitcast(F32), ALU.subtract).then_inc(olo_done, 1)

            def split_x2(b):
                dve.wait_ge(x2hi_done, b)
                nc.vector.tensor_tensor(x2_lo[:], ps_m[:, 0, :].rearrange("p (c q) -> p c q", c=DC),
                                        x2_hi[:].bitcast(F32), ALU.subtract).then_inc(x2lo_done, 1)

            def hidden(b, f):
                n = FC * (b - 1) + f
                dve.wait_ge(tanh_done, n + 1)
                if f >= 2:
                    dve.wait_ge(hlo_done, n - 1)
                nc.vector.scalar_tensor_tensor(hid[:, f % 2, :], tanh_g[:, f % 2, :], 1.0,
                                               ps_m[:, (f + 1) % 2, 0:Q], ALU.add, ALU.mult).then_inc(gated, 1)
                dve.wait_ge(gated, n + 1)
                nc.vector.tensor_tensor(hid[:, f % 2, :], hid[:, f % 2, :], ps_m[:, (f + 1) % 2, Q:2 * Q],
                                        ALU.mult).then_inc(hid_done, 1)

            def normalise_x(n):
                dve.wait_ge(xln_in, 16 * (n + 1))
                if not (isinstance(n, int) and n == 0):
                    dve.wait_ge(xt_done, n)
                for t in range(NT):
                    col = NT * n + t
                    at = slice(col, col + 1) if isinstance(n, int) else bass.ds(col, 1)
                    nc.vector.tensor_scalar(x_hat[:, t, :], x_ln[:, t, :], mean1[:, at], rstd1[:, at],
                                            ALU.subtract, ALU.mult).then_inc(xhat_done, 1)

            def result(b, t):
                dve.wait_ge(down_done, NT * (b - 1) + t + 1)
                nc.vector.scalar_tensor_tensor(x1[:, t, :], ps_m[:, (t + 1) % 2, 0:D], 0.5 * QUANT ** 3,
                                               x1[:, t, :], ALU.mult, ALU.add).then_inc(y_done, 1)

            def residual(b, t):
                dve.wait_ge(proj_done, NT * b + t + 1)
                if t == 0:
                    dve.wait_ge(xres_biased, b + 1)
                    wait(dve, y_out, 16 * b)
                nc.vector.scalar_tensor_tensor(x1[:, t, :], ps_m[:, t, 0:D], tgate[:, 0:1], x_res[:, t, :],
                                               ALU.mult, ALU.add).then_inc(x1_done, 1)
                dve.wait_ge(x1_done, NT * b + t + 1)
                nc.vector.bn_stats(stats[:, t, :], x1[:, t, :]).then_inc(stat_done, 1)

            def normalise_x1(b):
                done = [0]

                def step(ins):
                    done[0] += 1
                    ins.then_inc(ln_step, 1)
                    dve.wait_ge(ln_step, LN_STEPS * b + done[0])

                dve.wait_ge(stat_done, NT * (b + 1))
                nc.vector.memset(rstd[:], 0.0).then_inc(rstd_cleared, 1)
                for t in range(NT):
                    ins = nc.vector.bn_aggr(mv[:, t, :], stats[:, t, :])
                step(ins)
                step(nc.vector.tensor_scalar(var_eps[:], mv[:, :, 1], EPS, None, ALU.add))
                env["rsqrt"](dve, step, rstd[:], var_eps[:], tmp[:])
                assert done[0] == LN_STEPS
                wait(dve, x2t_done, b)
                for t in range(NT):
                    nc.vector.tensor_scalar(x1_hat[:, t, :], x1[:, t, :], mv[:, t, 0:1], rstd[:, t:t + 1],
                                            ALU.subtract, ALU.mult).then_inc(x1hat_done, 1)
                dve.wait_ge(x1hat_done, NT * (b + 1))

            normalise_x(0)

            def body(b, attn=True, ffn=True, more=True):
                if attn:
                    maxima(b, 0)
                if ffn:
                    split_x2(b)
                if attn:
                    maxima(b, 1)
                    sums(b, 0)
                if ffn:
                    hidden(b, 0)
                if attn:
                    sums(b, 1)
                    maxima(b, 2)
                if ffn:
                    hidden(b, 1)
                if attn:
                    sums(b, 2)
                if ffn:
                    hidden(b, 2)
                if attn:
                    maxima(b, 3)
                if ffn:
                    hidden(b, 3)
                if attn:
                    sums(b, 3)
                if ffn:
                    hidden(b, 4)
                if attn:
                    split_o(b, 0)
                if ffn:
                    hidden(b, 5)
                if more:
                    normalise_x(b + 1)
                if ffn:
                    result(b, 0)
                    result(b, 1)
                if attn:
                    split_o(b, 1)
                    residual(b, 0)
                    residual(b, 1)
                    normalise_x1(b)

            batches(dve, body)


_INS = ["x", "ctx_1024", "L0_xattn_ln_gamma", "L0_xattn_ln_beta", "L0_xattn_w_q", "L0_xattn_w_kv",
        "L0_xattn_w_out", "L0_xattn_b_out", "L0_xattn_gate", "L0_ffn_w_gate", "L0_ffn_w_up", "L0_ffn_w_down"]


def kernel(**inputs):
    import numpy as np
    import concourse.bacc as bacc
    from concourse.bass_utils import run_bass_kernel_spmd

    nc = bacc.Bacc("TRN2", target_bir_lowering=False, num_devices=1)
    arrays, args = {}, []
    for name in _INS:
        a = np.ascontiguousarray(inputs[name])
        arrays[f"in_{name}"] = a
        args.append(nc.dram_tensor(f"in_{name}", a.shape, mybir.dt.from_np(a.dtype), kind="ExternalInput").ap())
    shape = arrays["in_x"].shape
    args.append(nc.dram_tensor("out", shape, F32, kind="ExternalOutput").ap())
    xattn_ffn_kernel(nc, *args)
    r = run_bass_kernel_spmd(nc, [arrays], core_ids=[0])
    return r.results[0]["out"]
```

```python
from contextlib import ExitStack

import concourse.bass as bass
from concourse import mybir

F32 = mybir.dt.float32
F32R = mybir.dt.float32r
I32 = mybir.dt.int32
ACT = mybir.ActivationFunctionType
ALU = mybir.AluOpType
AXIS_X = mybir.AxisListType.X

P = 128
BANK = 512
HEADS = 16
EPS = 1e-5
RSQRT_SEED = 0x5F3759DF
HOISTED = 2
PE_ORDER = "S2 S3 T0 T1 X1T XT V0 G0 G1 T2 G2 G3 T3 G4 V1 G5 S0 S1 D0 D1 O0 O1".split()
DVE_ORDER = "M2 M3 LN1 LN Z2 X1 Z3 O0 H0 H1 H2 H3 H4 H5 O1 M0 Y0 Z0 Y1 M1 R0 Z1 R1 AG".split()
ACT_ORDER = "Ta C0 E2 C1 E3 X1 X O0 t0 t1 h0 C2 t2 h1 t3 C3 h2 Tb h3 t4 O1 t5 h4 h5 E0 E1".split()
POOL_ORDER = "Ta P2 X P3 h0 B h1 h2 h3 h4 h5 Tb P0 P1 LN".split()
SP_ORDER = "RES LN V OUT".split()
PE_START = "v0 v1 v2 XT v3 v4 v5 S0 v6 v7 S1 v8 v9 f0 f1 f2 f3 f4 f5 f6 f7 f8".split()
ACT_START = "Ta Tb X v3 v5 v4 v7 E0 v9 WO E1 f3 f4 f5".split()
DVE_START = "F0 F1 F2 LN v0 v1 v2 M0 v6 M1 v8 f0 Z0 f1 f2 Z1 f7 f8 f6".split()
POOL_START = "XS Ta X Tb WO P0 P1".split()
ACT_T = (0, 1, 3, 4, 5, 7)
WARM_UP = (8, 12)
STATS_PER_JOB = 2
QUANT = 1.0 / 127.0


def xattn_ffn_kernel(nc, x, ctx_in, ln_gamma, ln_beta, w_q, w_kv, w_out, b_out, gate,
                     w_gate, w_up, w_down, out):
    B, S, D = x.shape
    K = ctx_in.shape[1]
    INNER = w_q.shape[1]
    DH = INNER // HEADS
    HID = w_gate.shape[0]
    DC = D // P
    NT = S // P
    IC = INNER // P
    FC = HID // P
    HK = HEADS * K
    HG = HEADS // 2
    HB = HG // 2
    CR = B * K
    RC = (CR + P - 1) // P
    HALF = B // 2
    HC = HALF * K
    SCALE = DH ** -0.5
    NU = 2 * NT
    GK = HG * K
    BK = HB * K
    Q = NT * P
    WP = 4
    VS = 4
    LN_STEPS = 3 + 12
    X_STEPS = 4 + 12
    assert HB * K <= BANK and DC == 2 and NT == 2 and 2 * DH == P and RC == VS + 1 and K <= P

    x_dram = x.rearrange("b (t p) d -> p b t d", p=P)
    out_dram = out.rearrange("b (t p) d -> p b t d", p=P)
    ctx_rows = ctx_in.rearrange("b k d -> (b k) d")
    v_scratch = nc.dram_tensor("v_scratch", (CR, INNER), F32, kind="Internal").ap()

    whole, weights_in, parts_in, before_loop = ExitStack(), ExitStack(), ExitStack(), ExitStack()
    with whole:
        def sem(name):
            return whole.enter_context(nc.semaphore(name))

        def sb(name, shape, dt=F32, where=whole):
            return where.enter_context(nc.sbuf_tensor(name, shape, dt))

        wo_hi = sb("wo_hi", [P, IC, D], F32R)
        wo_lo = sb("wo_lo", [P, IC, D], F32R)
        wv_hi = wo_hi[:].rearrange("p i d -> p (i d)").rearrange("p (c n) -> p c n", c=DC)
        wv_lo = wo_lo[:].rearrange("p i d -> p (i d)").rearrange("p (c n) -> p c n", c=DC)
        ident = sb("ident", [P, P])
        gamma = sb("gamma", [P, DC])
        beta = sb("beta", [P, DC])
        tgate = sb("tgate", [P, 1])
        bias = sb("bias", [P, D])
        consts = sb("consts", [P, 3, B * NT])
        mean1 = sb("mean1", [P, B * NT])
        rstd1 = sb("rstd1", [P, B * NT])
        x_ln = sb("x_ln", [P, NT, D])
        x_hat = sb("x_hat", [P, NT, D])

        with weights_in:
            wv_raw = sb("wv_raw", [P, DC, INNER], where=weights_in)
            wqt_own = sb("wqt_own", [P, IC, D], F32R, where=weights_in)
            stats1 = sb("stats1", [P, 2, 6], where=weights_in)
            mv1 = sb("mv1", [P, B * NT, 2], where=weights_in)
            var1 = sb("var1", [P, B * NT], where=weights_in)
            half1 = sb("half1", [P, B * NT], where=weights_in)
            tmp1 = sb("tmp1", [P, B * NT], where=weights_in)
        wg = sb("wg", [P, DC, HID], F32R)
        wu = sb("wu", [P, DC, HID], F32R)
        wd = sb("wd", [P, FC, D], F32R)

        with parts_in:
            ctx_raw = sb("ctx_raw", [P, RC, D], where=parts_in)
            wk_raw = sb("wk_raw", [P, DC, INNER], where=parts_in)
            wk_hi = sb("wk_hi", [P, DC, INNER], F32R, where=parts_in)
            wk_lo = sb("wk_lo", [P, DC, INNER], F32R, where=parts_in)
            wq_raw = sb("wq_raw", [P, DC, INNER], where=parts_in)
        t_all = sb("t_all", [P, DC, B, HK])

        with before_loop:
            wqt_hi = sb("wqt_hi", [P, IC, 2, D], F32R, where=before_loop)
            wqt_lo = sb("wqt_lo", [P, IC, D], F32R, where=before_loop)
            kt = sb("kt", [P, HEADS, CR], F32R, where=before_loop)
            sb("gap", [P, 160], where=before_loop)
            wg_raw = sb("wg_raw", [P, FC, D], where=before_loop)
            wu_raw = sb("wu_raw", [P, FC, D], where=before_loop)
            wd_raw = sb("wd_raw", [P, DC, HID], where=before_loop)
            ct_hi = sb("ct_hi", [P, DC, CR], F32R, where=before_loop)
            ct_lo = sb("ct_lo", [P, DC, CR], F32R, where=before_loop)

        t_hi = sb("t_hi", [P, DC, HK], F32R)
        t_lo = sb("t_lo", [P, DC, HK], F32R)
        xn = sb("xn", [P, DC, Q])
        xn_hi = sb("xn_hi", [P, DC, Q], F32R)
        xn_lo = sb("xn_lo", [P, DC, Q], F32R)
        probs = sb("probs", [P, NU, GK])
        top = sb("top", [P, NU, HG])
        total = sb("total", [P, NU, HG])
        v = sb("v", [K, INNER])
        with ExitStack() as after_t:
            v_out = sb("v_out", [P, VS, INNER], where=after_t)
            wo_raw = sb("wo_raw", [P, IC, D], where=after_t)
        pt = sb("pt", [K, HG, Q])
        o_hi = sb("o_hi", [P, IC, Q], F32R)
        o_lo = sb("o_lo", [P, IC, Q], F32R)
        h_hi = sb("h_hi", [P, FC, Q], F32R)
        h_lo = sb("h_lo", [P, FC, Q], F32R)
        x1_hat = sb("x1_hat", [P, NT, D])
        x2_hi = sb("x2_hi", [P, DC, Q], F32R)
        x2_lo = sb("x2_lo", [P, DC, Q], F32R)
        tanh_g = sb("tanh_g", [P, 2, Q])
        hid = sb("hid", [P, 2, Q])
        x_res = sb("x_res", [P, NT, D])
        x1 = sb("x1", [P, NT, D])
        stats = sb("stats", [P, NT, 6])
        mv = sb("mv", [P, NT, 2])
        var_eps = sb("var_eps", [P, NT])
        half_var = sb("half_var", [P, NT])
        rstd = sb("rstd", [P, NT])
        tmp = sb("tmp", [P, NT])
        spare = sb("spare", [P, 1])
        spare_pool = sb("spare_pool", [P, NT])

        ps = whole.enter_context(nc.psum_tensor("ps", [P, 8, BANK], F32))
        ps_s = ps[:, 0:4, :].rearrange("p (u r) n -> p u r n", u=2)
        ps_p = ps[:, 4:6, :]
        ps_m = ps[:, 6:8, :]

        s_in = {n: sem(f"in_{n}") for n in "ctx wq wv wo wg wu wd small".split()}
        s_wk = [sem(f"in_wk_{i}") for i in range(WP)]
        s_xs = [sem(f"x_for_stats_{i}") for i in range(2)]
        s_dup = [sem(f"wq_hi_doubled_{i}") for i in range(2)]
        s_vfirst, s_vrest = sem("v_first_rows_stored"), sem("v_other_rows_stored")
        s_ident0, s_ident = sem("ident_zeroed"), sem("ident_ready")
        s_job = sem("job_done")
        s_act, s_dve = sem("job_copied_by_act"), sem("job_copied_by_dve")
        s_wkh, s_wkl = sem("wk_hi_ready"), sem("wk_lo_ready")
        s_wvh, s_wvl = sem("wv_hi_ready"), sem("wv_lo_ready")
        s_woh, s_wol = sem("wo_hi_ready"), sem("wo_lo_ready")
        s_float = sem("ints_made_float")
        s_tgate, s_bias = sem("tanh_gate_ready"), sem("bias_ready")
        s_stat, s_aggr, s_ln = sem("x_stats_done"), sem("x_aggr_done"), sem("x_norm_step")
        xln_in, xres_in, v_in, y_out = sem("xln_in"), sem("xres_in"), sem("v_in"), sem("y_out")
        scores_done, pt_done, pv_done = sem("scores_done"), sem("pt_done"), sem("pv_done")
        xt_done, x2t_done, gu_done = sem("xt_done"), sem("x2t_done"), sem("gu_done")
        down_done, proj_done = sem("down_done"), sem("proj_done")
        max_done, sub_done, sum_done, rec_done = sem("max_done"), sem("sub_done"), sem("sum_done"), sem("rec_done")
        olo_done, x2lo_done, gated, hid_done = sem("olo_done"), sem("x2lo_done"), sem("gated"), sem("hid_done")
        x1_done, stat_done, ln_step, x1hat_done = sem("x1_done"), sem("stat_done"), sem("ln_step"), sem("x1hat_done")
        aggr_done, spare_cleared = sem("aggr_done"), sem("spare_cleared")
        consts_set = sem("consts_set")
        xhat_done, y_done = sem("xhat_done"), sem("y_done")
        exp_done, pt_copied, ohi_done = sem("exp_done"), sem("pt_copied"), sem("ohi_done")
        thi_done, tanh_done, hhi_done = sem("thi_done"), sem("tanh_done"), sem("hhi_done")
        x2hi_done, xn_done, xnhi_done = sem("x2hi_done"), sem("xn_done"), sem("xnhi_done")
        probs_done, tlo_done, hlo_done = sem("probs_done"), sem("tlo_done"), sem("hlo_done")
        xres_biased, xnlo_done = sem("xres_biased"), sem("xnlo_done")

        shared = [n for n in PE_ORDER if n in ("X1T", "XT", "G0", "G1", "G2", "G3", "G4", "G5", "D0", "D1", "O0", "O1")]
        bank = {n: i % 2 for i, n in enumerate(shared)}

        def last_user(b, name):
            at = shared.index(name) - 2
            while at >= 0:
                n, k = shared[at], int(shared[at][1]) if shared[at][1].isdigit() else 0
                if n == "XT" and not (isinstance(b, int) and b >= B - 1):
                    return xn_done, DC * (b + 2)
                if n[0] == "O" and not (isinstance(b, int) and b == B):
                    return x1_done, NT * b + k + 1
                if not (isinstance(b, int) and b == 0):
                    if n == "X1T":
                        return x2lo_done, b
                    if n[0] == "G":
                        return hid_done, FC * (b - 1) + k + 1
                    if n[0] == "D":
                        return y_done, NT * (b - 1) + k + 1
                at -= 2
            return None

        def wait(eng, s, value):
            if isinstance(value, int) and value <= 0:
                return
            eng.wait_ge(s, value)


        jobs = [("ctx", r) for r in range(RC)]
        for step in "k0 k1 k2 w0 w1 k3 k4 w2 w3 k5 k6 k7".split():
            jobs += [("k" if step[0] == "k" else "wq", int(step[1:]))]
        jobs += [("t", h, n) for h in range(HEADS) for n in range(2)]
        first_t, last_t = jobs.index(("t", 0, 0)), len(jobs) - 1
        first_v = len(jobs)
        jobs += [("v", r, n) for r in range(RC) for n in range(2)]
        last_v = len(jobs) - 1
        first_f = len(jobs)
        jobs += [(w, f) for w in ("wg", "wu", "wd") for f in range(FC // 2)]
        other = 6 + 1 - bank["XT"]

        def banks_of(n):
            j = jobs[n]
            if j[0] == "ctx":
                return [j[1]]
            if j[0] == "k":
                at = 2 * ((j[1] + 1) % 3)
                return [at, at + 1]
            if j[0] == "wq":
                return [6 + j[1] % 2]
            if j[0] == "t":
                at = 2 * ((n - first_t) % 4)
                return [at, at + 1]
            return [(4, 5, other)[(n - first_v) % 3]]

        def job_of(token):
            if token[0] in "vf" and token[1:].isdigit():
                return (first_v if token[0] == "v" else first_f) + int(token[1:])

        act_t = {first_t + i for i in range(2 * HEADS) if i % 8 in ACT_T}
        both = [n for n in range(first_t)]
        act_jobs = both + sorted(act_t) + [job_of(s) for s in ACT_START if job_of(s) is not None]
        dve_jobs = both + [n for n in range(first_t, first_v) if n not in act_t]
        dve_jobs += [job_of(s) for s in DVE_START if job_of(s) is not None]
        by_act = {n: i + 1 for i, n in enumerate(act_jobs)}
        by_dve = {n: i + 1 for i, n in enumerate(dve_jobs)}
        holder, before = {}, []
        for n in range(len(jobs)):
            before.append(sorted({holder[k] for k in banks_of(n) if k in holder}))
            holder.update({k: n for k in banks_of(n)})

        def evacuated(eng, n):
            if n in by_act:
                eng.wait_ge(s_act, by_act[n])
            if n in by_dve:
                eng.wait_ge(s_dve, by_dve[n])

        def rows(r):
            return min(P, CR - r * P)

        def psum_of(n):
            j, b = jobs[n], banks_of(n)[0]
            if j[0] == "ctx":
                return ps[:, b, 0:DC * P].rearrange("p (c r) -> p c r", c=DC)[:, :, 0:rows(j[1])]
            if j[0] == "v":
                return ps[0:rows(j[1]), b, :]
            if j[0] == "k":
                return ps[:, b:b + 2, 0:HC]
            if j[0] == "t":
                return ps[:, b:b + 2, 0:HC].rearrange("p c (b k) -> p c b k", k=K)
            return ps[:, b, :].rearrange("p (c r) -> p c r", c=2)

        def target(n):
            j = jobs[n]
            if j[0] == "v":
                return v_out[0:rows(j[1]), j[1] % VS, j[2] * BANK:(j[2] + 1) * BANK]
            if j[0] == "wg":
                return wg[:, :, j[1] * 2 * P:(j[1] + 1) * 2 * P]
            if j[0] == "wu":
                return wu[:, :, j[1] * 2 * P:(j[1] + 1) * 2 * P]
            if j[0] == "wd":
                return wd[:, 2 * j[1]:2 * j[1] + 2, :]
            return t_all[:, :, j[2] * HALF:(j[2] + 1) * HALF, j[1] * K:(j[1] + 1) * K]

        def parts(n):
            j = jobs[n]
            if j[0] == "ctx":
                cols = slice(j[1] * P, j[1] * P + rows(j[1]))
                return [(psum_of(n), ct_hi[:, :, cols], ct_lo[:, :, cols])]
            halves = [slice(0, DH), slice(DH, P)]
            if j[0] == "k":
                return [(psum_of(n)[halves[e]], kt[halves[e], 2 * j[1] + e, :].rearrange("p (n c) -> p n c", n=2),
                         kt[halves[1 - e], 2 * j[1] + e, :].rearrange("p (n c) -> p n c", n=2)) for e in range(2)]
            pairs = slice(2 * j[1], 2 * j[1] + 2)
            return [(psum_of(n), wqt_own[:, pairs, :], wqt_lo[:, pairs, :])]

        def rsqrt(step, carry, r, v, half, tmp):
            tt = nc.gpsimd.tensor_tensor
            n = v.shape[1]
            step(tt(half, v, consts[:, 1, 0:n], ALU.mult))
            carry()
            step(nc.gpsimd.tensor_scalar(r.bitcast(I32), v.bitcast(I32), -0.5, RSQRT_SEED, ALU.mult, ALU.add))
            for _ in range(3):
                step(tt(tmp, r, r, ALU.mult))
                step(tt(tmp, tmp, half, ALU.mult))
                step(tt(tmp, tmp, consts[:, 2, 0:n], ALU.add))
                step(tt(r, tmp, r, ALU.mult))

        def batches(eng, start, order, stages):
            def body(b, now=True, ffn=True, nxt=True):
                for name in order:
                    part, fn, *args = stages[name]
                    if part == "now" and now:
                        fn(b, *args)
                    if part == "ffn" and ffn:
                        fn(b, *args)
                    if part == "next" and nxt:
                        fn(b + 1, *args)

            for name in start:
                part, fn, *args = stages.get(name, (None, None))
                if part == "start":
                    fn(*args)
                elif part == "next":
                    fn(0, *args)
                else:
                    stages["job"](job_of(name))
            body(0, ffn=False)
            with eng.Fori(1, B - 1) as b:
                body(b)
            body(B - 1, nxt=False)
            body(B, now=False, nxt=False)

        block = whole.enter_context(nc.Block())

        @block.sync
        def _(sp):
            def load_res(b):
                if isinstance(b, int) and b == 0:
                    sp.wait_ge(s_job, last_v + 1)
                wait(sp, x1_done, NT * b)
                sp.dma_start(x_res[:], x_dram[:, b]).then_inc(xres_in, 16)

            def load_ln(n):
                wait(sp, xhat_done, NT * n)
                sp.dma_start(x_ln[:], x_dram[:, n]).then_inc(xln_in, 16)

            def store(b):
                sp.wait_ge(y_done, NT * b)
                sp.dma_start(out_dram[:, b - 1], x1[:]).then_inc(y_out, 16)

            def load_v(n):
                if isinstance(n, int) and n == 1:
                    sp.wait_ge(s_vrest, 16 * (RC - 1))
                wait(sp, pv_done, NU * n)
                sp.dma_start(v[:], v_scratch.rearrange("(b k) n -> b k n", k=K)[n]).then_inc(v_in, 16)

            sp.dma_start(ctx_raw[:, 0:RC - 1, :],
                         ctx_rows[0:(RC - 1) * P, :].rearrange("(r p) d -> p r d", p=P)).then_inc(s_in["ctx"], 16)
            sp.dma_start(ctx_raw[0:rows(RC - 1), RC - 1, :], ctx_rows[(RC - 1) * P:CR, :]).then_inc(s_in["ctx"], 16)
            w_kv_rows = w_kv.rearrange("(c p) n -> p c n", p=P)
            for i in range(WP):
                cols = slice(i * INNER // WP, (i + 1) * INNER // WP)
                sp.dma_start(wk_raw[:, :, cols], w_kv_rows[:, :, cols]).then_inc(s_wk[i], 16)
                if i == 0:
                    sp.dma_start(wq_raw[:], w_q.rearrange("(c p) n -> p c n", p=P)).then_inc(s_in["wq"], 16)
            sp.dma_start(wv_raw[:], w_kv_rows[:, :, INNER:2 * INNER]).then_inc(s_in["wv"], 16)
            for name, raw, w in (("wg", wg_raw, w_gate), ("wu", wu_raw, w_up), ("wd", wd_raw, w_down)):
                sp.dma_start(raw[:].bitcast(I32), w.rearrange("(r p) n -> p r n", p=P)).then_inc(s_in[name], 16)
            for b in range(B - 1, -1, -1):
                if b == B - 3:
                    for i in range(2):
                        sp.wait_ge(s_act, by_act[jobs.index(("wq", 2 * i + 1))])
                        pairs = slice(4 * i, 4 * i + 4)
                        for e in range(2):
                            for to in range(2):
                                sp.dma_start(wqt_hi[to * DH:(to + 1) * DH, pairs, e, :].bitcast(F32),
                                             wqt_own[e * DH:(e + 1) * DH, pairs, :].bitcast(F32)).then_inc(s_dup[i], 16)
                if b < B - 2:
                    sp.wait_ge(s_stat, NT * (B - 2 - b))
                sp.dma_start((x_hat if b % 2 else x_ln)[:], x_dram[:, b]).then_inc(xln_in if b == 0 else s_xs[b % 2], 16)
            sp.wait_ge(s_job, last_t + 1)
            sp.dma_start(wo_raw[:], w_out.rearrange("(i p) n -> p i n", p=P)).then_inc(s_in["wo"], 16)
            for r in range(RC):
                for n in range(2):
                    evacuated(sp, first_v + 2 * r + n)
                sp.dma_start(v_scratch[r * P:r * P + rows(r), :],
                             v_out[0:rows(r), r % VS, :]).then_inc(s_vfirst if r == 0 else s_vrest, 16)
                if r == 1:
                    sp.wait_ge(s_vfirst, 16)
                    load_v(0)

            batches(sp, [], SP_ORDER, {"RES": ("now", load_res), "LN": ("next", load_ln),
                                   "OUT": ("ffn", store), "V": ("next", load_v)})
            sp.wait_ge(y_out, 16 * B)

        @block.tensor
        def _(pe):
            mm = nc.tensor.matmul

            def job(n):
                j = jobs[n]
                kind = j[0]
                for m in before[n]:
                    evacuated(pe, m)
                o = psum_of(n)
                if kind == "ctx":
                    m = rows(j[1])
                    for c in range(DC):
                        ins = nc.tensor.transpose(o[:, c, :], ctx_raw[0:m, j[1], c * P:(c + 1) * P], ident[0:m, 0:m])
                if kind == "k":
                    i = j[1]
                    if i == 0:
                        evacuated(pe, RC - 1)
                    if i % (IC // WP) == 0:
                        pe.wait_ge(s_wkl, i // (IC // WP) + 1)
                    ws = slice(i * P, (i + 1) * P)
                    for n2 in range(2):
                        cols = slice(n2 * HC, (n2 + 1) * HC)
                        for c in range(DC):
                            mm(o[:, n2, :], wk_hi[:, c, ws], ct_hi[:, c, cols], start=c == 0, stop=False)
                            mm(o[:, n2, :], wk_hi[:, c, ws], ct_lo[:, c, cols], start=False, stop=False)
                            ins = mm(o[:, n2, :], wk_lo[:, c, ws], ct_hi[:, c, cols], start=False, stop=c == DC - 1)
                if kind == "wq":
                    if j[1] == 0:
                        pe.wait_ge(s_in["wq"], 16)
                    for a in range(2):
                        i = 2 * j[1] + a
                        for c in range(DC):
                            ins = nc.tensor.transpose(o[:, a, c * P:(c + 1) * P],
                                                      wq_raw[:, c, i * P:(i + 1) * P], ident[:])
                if kind == "t":
                    h, half = j[1:]
                    if half == 0:
                        evacuated(pe, jobs.index(("k", h // 2)))
                        evacuated(pe, jobs.index(("wq", h // 4)))
                        pe.wait_ge(s_dup[h // 8], 64)
                    i, ds = h // 2, slice((h % 2) * DH, (h % 2 + 1) * DH)
                    cols = slice(half * HC, (half + 1) * HC)
                    for c in range(DC):
                        oc = ps[:, banks_of(n)[c], 0:HC]
                        ws = slice(c * P, (c + 1) * P)
                        mm(oc, wqt_hi[:, i, h % 2, ws], kt[:, h, cols], start=True, stop=False)
                        ins = mm(oc, wqt_lo[ds, i, ws], kt[ds, h, cols], start=False, stop=True)
                if kind == "v":
                    if n == first_v:
                        pe.wait_ge(s_wvl, 1)
                    cols = slice(j[2] * BANK, (j[2] + 1) * BANK)
                    rs = slice(j[1] * P, j[1] * P + rows(j[1]))
                    for c in range(DC):
                        mm(o, ct_hi[:, c, rs], wv_hi[:, c, cols], start=c == 0, stop=False)
                        mm(o, ct_hi[:, c, rs], wv_lo[:, c, cols], start=False, stop=False)
                        ins = mm(o, ct_lo[:, c, rs], wv_hi[:, c, cols], start=False, stop=c == DC - 1)
                if kind in ("wg", "wu", "wd"):
                    if j[1] == 0:
                        pe.wait_ge(s_float, ("wg", "wu", "wd").index(kind) + 1)
                    for a in range(2):
                        for c in range(2):
                            if kind == "wd":
                                f = 2 * j[1] + a
                                ins = nc.tensor.transpose(o[:, a, c * P:(c + 1) * P],
                                                          wd_raw[:, c, f * P:(f + 1) * P], ident[:])
                            else:
                                raw = wg_raw if kind == "wg" else wu_raw
                                ins = nc.tensor.transpose(o[:, c, a * P:(a + 1) * P],
                                                          raw[:, 2 * j[1] + a, c * P:(c + 1) * P], ident[:])
                ins.then_inc(s_job, 1)

            def warm_up(times):
                for _ in range(times):
                    mm(ps[:, 7, 0:P], ident[:], ident[:], start=True, stop=True)

            pe.wait_ge(s_ident, 1)
            warm_up(WARM_UP[0])
            pe.wait_ge(s_in["ctx"], 32)
            for n in range(first_v):
                job(n)
                if n == RC - 1:
                    warm_up(WARM_UP[1])

            def claim(b, name):
                if isinstance(b, int) and b < 0:
                    return
                user = last_user(b, name)
                if user:
                    pe.wait_ge(*user)

            def scores(b, u):
                g, t = divmod(u, NT)
                if u == 0:
                    pe.wait_ge(xnhi_done, b + 1)
                    pe.wait_ge(xnlo_done, b + 1)
                if t == 0:
                    pe.wait_ge(tlo_done, 2 * b + g + 1)
                wait(pe, sub_done, NU * b + u - 1)
                qs = slice(t * P, (t + 1) * P)
                for r in range(2):
                    o = ps_s[:, u % 2, r, 0:BK]
                    cols = slice((g * HG + r * HB) * K, (g * HG + (r + 1) * HB) * K)
                    for c in range(DC):
                        mm(o, xn_hi[:, c, qs], t_hi[:, c, cols], start=c == 0, stop=False)
                        mm(o, xn_hi[:, c, qs], t_lo[:, c, cols], start=False, stop=False)
                        ins = mm(o, xn_lo[:, c, qs], t_hi[:, c, cols], start=False, stop=c == DC - 1)
                ins.then_inc(scores_done, 1)

            def transpose_probs(b, g, t):
                u = NT * g + t
                pe.wait_ge(probs_done, NU * b + u + 1)
                if isinstance(b, int) and b == 0 and u == 0:
                    for n in range(len(jobs) - 3, len(jobs)):
                        evacuated(pe, n)
                for q in range(2):
                    m = 2 * t + q
                    if m < 2:
                        wait(pe, olo_done, NU * b + 2 * g + m - 1)
                    else:
                        pe.wait_ge(pt_copied, 8 * b + 4 * g + m - 1)
                    for h in range(HB):
                        hh = q * HB + h
                        ins = nc.tensor.transpose(ps_p[0:K, m % 2, h * P:(h + 1) * P],
                                                  probs[:, u, hh * K:(hh + 1) * K], ident[:])
                    ins.then_inc(pt_done, 1)

            def values(b, g):
                pe.wait_ge(pt_copied, 8 * b + 4 * g + 4)
                if g == 0:
                    pe.wait_ge(v_in, 16 * (b + 1))
                for i in range(2):
                    for pair in range(2):
                        for e in range(2):
                            h = 4 * i + 2 * pair + e
                            gh = g * HG + h
                            ins = mm(ps_p[e * DH:(e + 1) * DH, i, pair * Q:(pair + 1) * Q],
                                     v[:, gh * DH:(gh + 1) * DH], pt[:, h, :], start=True, stop=True)
                    ins.then_inc(pv_done, 1)

            def transpose_x(n):
                pe.wait_ge(xhat_done, NT * (n + 1))
                if isinstance(n, int) and n == 0:
                    evacuated(pe, last_t)
                claim(n - 1, "XT")
                for c in range(DC):
                    for t in range(NT):
                        ins = nc.tensor.transpose(ps_m[:, bank["XT"], c * Q + t * P:c * Q + (t + 1) * P],
                                                  x_hat[:, t, c * P:(c + 1) * P], ident[:])
                ins.then_inc(xt_done, 1)

            def transpose_x1(b):
                pe.wait_ge(x1hat_done, NT * b)
                for c in range(DC):
                    for t in range(NT):
                        ins = nc.tensor.transpose(ps_m[:, bank["X1T"], c * Q + t * P:c * Q + (t + 1) * P],
                                                  x1_hat[:, t, c * P:(c + 1) * P], ident[:])
                ins.then_inc(x2t_done, 1)

            def gate_up(b, f):
                if f == 0:
                    pe.wait_ge(x2hi_done, b)
                    pe.wait_ge(x2lo_done, b)
                claim(b, f"G{f}")
                fs = slice(f * P, (f + 1) * P)
                for w, at in ((wg, 0), (wu, Q)):
                    o = ps_m[:, bank[f"G{f}"], at:at + Q]
                    for c in range(DC):
                        mm(o, w[:, c, fs], x2_hi[:, c, :], start=c == 0, stop=False)
                        ins = mm(o, w[:, c, fs], x2_lo[:, c, :], start=False, stop=c == DC - 1)
                ins.then_inc(gu_done, 1)

            def down(b, t):
                if t == 0:
                    pe.wait_ge(hhi_done, FC * b)
                    pe.wait_ge(hlo_done, FC * b)
                claim(b, f"D{t}")
                o = ps_m[:, bank[f"D{t}"], 0:D]
                ts = slice(t * P, (t + 1) * P)
                for f in range(FC):
                    mm(o, h_hi[:, f, ts], wd[:, f, :], start=f == 0, stop=False)
                    ins = mm(o, h_lo[:, f, ts], wd[:, f, :], start=False, stop=f == FC - 1)
                ins.then_inc(down_done, 1)

            def project(b, t):
                if isinstance(b, int) and b == 0 and t == 0:
                    pe.wait_ge(s_wol, 1)
                if t == 0:
                    pe.wait_ge(ohi_done, NU * (b + 1))
                    pe.wait_ge(olo_done, NU * (b + 1))
                claim(b, f"O{t}")
                o = ps_m[:, bank[f"O{t}"], 0:D]
                ts = slice(t * P, (t + 1) * P)
                for i in range(IC):
                    mm(o, o_hi[:, i, ts], wo_hi[:, i, :], start=i == 0, stop=False)
                    mm(o, o_hi[:, i, ts], wo_lo[:, i, :], start=False, stop=False)
                    ins = mm(o, o_lo[:, i, ts], wo_hi[:, i, :], start=False, stop=i == IC - 1)
                ins.then_inc(proj_done, 1)

            stages = {"X1T": ("ffn", transpose_x1), "XT": ("next", transpose_x)}
            for u in range(NU):
                stages[f"S{u}"] = ("next" if u < HOISTED else "now", scores, u)
                stages[f"T{u}"] = ("now", transpose_probs, u // NT, u % NT)
            for t in range(NT):
                stages[f"V{t}"] = ("now", values, t)
                stages[f"D{t}"] = ("ffn", down, t)
                stages[f"O{t}"] = ("now", project, t)
            for f in range(FC):
                stages[f"G{f}"] = ("ffn", gate_up, f)
            stages["job"] = job
            batches(pe, PE_START, PE_ORDER, stages)

        @block.scalar
        def _(act):
            act.dma_start(gamma[:], ln_gamma.rearrange("(c p) -> p c", p=P),
                          allow_slow_non_contiguous=True).then_inc(s_in["small"], 16)
            act.dma_start(beta[:], ln_beta.rearrange("(c p) -> p c", p=P),
                          allow_slow_non_contiguous=True).then_inc(s_in["small"], 16)
            act.dma_start(tgate[:], gate.rearrange("(a n) -> a n", a=1).to_broadcast([P, 1])).then_inc(s_in["small"], 16)
            act.dma_start(bias[:], b_out.rearrange("(a n) -> a n", a=1).to_broadcast([P, D])).then_inc(s_in["small"], 16)

            def copy(n):
                act.wait_ge(s_job, n + 1)
                if n < first_t:
                    for part in parts(n):
                        ins = nc.scalar.copy(part[1], part[0])
                    ins.then_inc(s_act, 1)
                else:
                    if jobs[n][0] == "v" and jobs[n][1] == VS:
                        act.wait_ge(s_vfirst, 16)
                    nc.scalar.copy(target(n), psum_of(n)).then_inc(s_act, 1)

            def wk_part(i):
                cols = slice(i * INNER // WP, (i + 1) * INNER // WP)
                act.wait_ge(s_wk[i], 16)
                nc.scalar.copy(wk_hi[:, :, cols], wk_raw[:, :, cols]).then_inc(s_wkh, 1)

            def wout_hi():
                act.wait_ge(s_in["wo"], 16)
                act.wait_ge(s_job, last_v + 1)
                nc.scalar.copy(wo_hi[:], wo_raw[:]).then_inc(s_woh, 1)

            for n in act_jobs:
                if n < first_v:
                    copy(n)
                if jobs[n] == ("ctx", RC - 1):
                    for i in range(WP // 2):
                        wk_part(i)
                if jobs[n][0] == "k" and jobs[n][1] < WP // 2:
                    wk_part(jobs[n][1] + WP // 2)
                if n == first_t - 1:
                    act.wait_ge(s_in["small"], 64)
                    nc.scalar.activation(tgate[:], tgate[:], ACT.Tanh).then_inc(s_tgate, 1)

            def exponentials(b, u):
                act.wait_ge(sub_done, NU * b + u + 1)
                nc.scalar.activation(probs[:, u, :], probs[:, u, :], ACT.Exp, scale=SCALE).then_inc(exp_done, 1)

            def copy_pt(b, g, t):
                for q in range(2):
                    m = 4 * g + 2 * t + q
                    act.wait_ge(pt_done, 8 * b + m + 1)
                    if t == 0 and q == 0:
                        wait(act, pv_done, NU * b + 2 * g)
                        if isinstance(b, int) and b == 0 and g == 0:
                            act.wait_ge(s_vrest, 16 * (RC - 1))
                    nc.scalar.copy(pt[:, q * HB:(q + 1) * HB, t * P:(t + 1) * P],
                                   ps_p[0:K, m % 2, :].rearrange("k (h q) -> k h q", h=HB)).then_inc(pt_copied, 1)

            def copy_o(b, g):
                for i in range(2):
                    n = 2 * g + i
                    act.wait_ge(pv_done, NU * b + n + 1)
                    if n == 0:
                        wait(act, proj_done, NT * b)
                    nc.scalar.copy(o_hi[:, 2 * n:2 * n + 2, :],
                                   ps_p[:, i, :].rearrange("p (i q) -> p i q", i=2)).then_inc(ohi_done, 1)

            def split_t(n, g):
                if isinstance(n, int) and n == 0:
                    act.wait_ge(s_job, last_t + 1)
                    act.wait_ge(s_dve, max(by_dve[m] for m in by_dve if m <= last_t))
                    act.wait_ge(s_act, max(by_act[m] for m in by_act if m <= last_t))
                if not (isinstance(n, int) and n == 0):
                    act.wait_ge(scores_done, NU * (n - 1) + NT * (g + 1))
                    act.wait_ge(tlo_done, 2 * (n - 1) + g + 1)
                nc.scalar.copy(t_hi[:, :, g * GK:(g + 1) * GK],
                               t_all[:, :, n, g * GK:(g + 1) * GK]).then_inc(thi_done, 1)

            def affine_x(n):
                act.wait_ge(xt_done, n + 1)
                if not (isinstance(n, int) and n == 0):
                    act.wait_ge(xnhi_done, n)
                    act.wait_ge(xnlo_done, n)
                for c in range(DC):
                    nc.scalar.activation(xn[:, c, :], ps_m[:, bank["XT"], c * Q:(c + 1) * Q], ACT.Identity,
                                         scale=gamma[:, c:c + 1], bias=beta[:, c:c + 1]).then_inc(xn_done, 1)
                act.wait_ge(xn_done, DC * (n + 1))
                if not (isinstance(n, int) and n == 0):
                    act.wait_ge(scores_done, NU * n)
                nc.scalar.copy(xn_hi[:], xn[:]).then_inc(xnhi_done, 1)

            def split_x2(b):
                act.wait_ge(x2t_done, b)
                nc.scalar.copy(x2_hi[:], ps_m[:, bank["X1T"], :].rearrange("p (c q) -> p c q", c=DC)).then_inc(x2hi_done, 1)

            def tanh(b, f):
                act.wait_ge(gu_done, FC * (b - 1) + f + 1)
                if f >= 2:
                    act.wait_ge(gated, FC * (b - 1) + f - 1)
                nc.scalar.activation(tanh_g[:, f % 2, :], ps_m[:, bank[f"G{f}"], 0:Q], ACT.Tanh,
                                     scale=QUANT / 2).then_inc(tanh_done, 1)

            def split_h(b, f):
                act.wait_ge(hid_done, FC * (b - 1) + f + 1)
                nc.scalar.copy(h_hi[:, f, :], hid[:, f % 2, :]).then_inc(hhi_done, 1)

            stages = {"X1": ("ffn", split_x2), "X": ("next", affine_x),
                      "Ta": ("next", split_t, 0), "Tb": ("next", split_t, 1)}
            for u in range(NU):
                stages[f"E{u}"] = ("next" if u < HOISTED else "now", exponentials, u)
                stages[f"C{u}"] = ("now", copy_pt, u // NT, u % NT)
            for g in range(2):
                stages[f"O{g}"] = ("now", copy_o, g)
            for f in range(FC):
                stages[f"t{f}"] = ("ffn", tanh, f)
                stages[f"h{f}"] = ("ffn", split_h, f)
            stages["job"], stages["WO"] = copy, ("start", wout_hi)
            batches(act, ACT_START, ACT_ORDER, stages)

        @block.gpsimd
        def _(pool):
            nc.gpsimd.memset(ident[:], 0.0).then_inc(s_ident0, 1)
            pool.wait_ge(s_ident0, 1)
            nc.gpsimd.affine_select(out=ident[:], in_=ident[:], compare_op=ALU.not_equal, fill=1.0,
                                    base=0, pattern=[[-1, P]], channel_multiplier=1).then_inc(s_ident, 1)
            for i, value in enumerate((EPS, -0.5, 1.5)):
                nc.gpsimd.memset(consts[:, i, :], value).then_inc(consts_set, 1)
            for i in range(WP):
                cols = slice(i * INNER // WP, (i + 1) * INNER // WP)
                pool.wait_ge(s_wkh, i + 1)
                nc.gpsimd.tensor_tensor(wk_lo[:, :, cols], wk_raw[:, :, cols], wk_hi[:, :, cols].bitcast(F32),
                                        ALU.subtract).then_inc(s_wkl, 1)
            pool.wait_ge(s_in["wv"], 16)
            nc.gpsimd.tensor_copy(wv_hi, wv_raw[:]).then_inc(s_wvh, 1)
            pool.wait_ge(s_wvh, 1)
            nc.gpsimd.tensor_tensor(wv_lo, wv_raw[:], wv_hi.bitcast(F32), ALU.subtract).then_inc(s_wvl, 1)
            steps = [0]

            def step(ins):
                steps[0] += 1
                ins.then_inc(s_ln, 1)
                if steps[0] < X_STEPS:
                    pool.wait_ge(s_ln, steps[0])

            def nothing():
                pass

            def x_scales():
                pool.wait_ge(consts_set, 3)
                pool.wait_ge(s_aggr, B * NT)
                tt = nc.gpsimd.tensor_tensor
                step(nc.gpsimd.tensor_copy(mean1[:], mv1[:, :, 0]))
                step(nc.gpsimd.tensor_scalar(var1[:], mv1[:, :, 1], 1.0 + EPS, EPS * EPS, ALU.mult, ALU.add))
                rsqrt(step, nothing, rstd1[:], var1[:], half1[:], tmp1[:])
                assert steps[0] == X_STEPS

            def wout_lo():
                pool.wait_ge(s_woh, 1)
                nc.gpsimd.tensor_tensor(wo_lo[:], wo_raw[:], wo_hi[:].bitcast(F32), ALU.subtract).then_inc(s_wol, 1)

            def normalise(b, u):
                pool.wait_ge(rec_done, NU * b + u + 1)
                p = probs[:, u, :].rearrange("p (h k) -> p h k", k=K)
                nc.gpsimd.tensor_tensor(p, p, total[:, u, :].unsqueeze(2).to_broadcast([P, HG, K]),
                                        ALU.mult).then_inc(probs_done, 1)

            def split_t(n, g):
                pool.wait_ge(thi_done, 2 * n + g + 1)
                cols = slice(g * GK, (g + 1) * GK)
                nc.gpsimd.tensor_tensor(t_lo[:, :, cols], t_all[:, :, n, cols], t_hi[:, :, cols].bitcast(F32),
                                        ALU.subtract).then_inc(tlo_done, 1)

            def split_xn(n):
                pool.wait_ge(xnhi_done, n + 1)
                nc.gpsimd.tensor_tensor(xn_lo[:], xn[:], xn_hi[:].bitcast(F32), ALU.subtract).then_inc(xnlo_done, 1)

            def split_h(b, f):
                pool.wait_ge(hhi_done, FC * (b - 1) + f + 1)
                nc.gpsimd.tensor_tensor(h_lo[:, f, :], hid[:, f % 2, :], h_hi[:, f, :].bitcast(F32),
                                        ALU.subtract).then_inc(hlo_done, 1)

            def norm_scale(b):
                if isinstance(b, int) and b == B - 1:
                    return
                done = [0]
                pool.wait_ge(aggr_done, NT * (b + 1))

                def step(ins):
                    done[0] += 1
                    ins.then_inc(ln_step, 1)
                    if done[0] < LN_STEPS:
                        pool.wait_ge(ln_step, LN_STEPS * b + done[0])

                def carry():
                    nc.gpsimd.tensor_tensor(spare_pool[:], consts[:, 0, 0:NT], consts[:, 1, 0:NT], ALU.mult)

                step(nc.gpsimd.tensor_tensor(var_eps[:], mv[:, :, 1], consts[:, 0, 0:NT], ALU.add))
                rsqrt(step, carry, rstd[:], var_eps[:], half_var[:], tmp[:])
                assert done[0] == LN_STEPS

            def bias_x(b):
                if isinstance(b, int) and b == 0:
                    pool.wait_ge(s_bias, 1)
                pool.wait_ge(xres_in, 16 * (b + 1))
                nc.gpsimd.tensor_tensor(x_res[:], x_res[:], bias[:].unsqueeze(1).to_broadcast([P, NT, D]),
                                        ALU.add).then_inc(xres_biased, 1)

            stages = {"Ta": ("next", split_t, 0), "Tb": ("next", split_t, 1), "B": ("now", bias_x), "X": ("next", split_xn), "LN": ("now", norm_scale)}
            for u in range(NU):
                stages[f"P{u}"] = ("next" if u < HOISTED else "now", normalise, u)
            for f in range(FC):
                stages[f"h{f}"] = ("ffn", split_h, f)
            stages["XS"], stages["WO"] = ("start", x_scales), ("start", wout_lo)
            batches(pool, POOL_START, POOL_ORDER, stages)

        @block.vector
        def _(dve):
            def copy(n):
                dve.wait_ge(s_job, n + 1)
                if n < first_t:
                    dve.wait_ge(s_act, by_act[n])
                    for psum, hi, lo in parts(n):
                        ins = nc.vector.tensor_tensor(lo, psum, hi.bitcast(F32), ALU.subtract)
                    ins.then_inc(s_dve, 1)
                else:
                    if jobs[n][0] == "v" and jobs[n][1] == VS:
                        dve.wait_ge(s_vfirst, 16)
                    nc.vector.tensor_copy(target(n), psum_of(n)).then_inc(s_dve, 1)

            def stat(i):
                b, t = B - 1 - i // NT, i % NT
                if b == 0:
                    dve.wait_ge(xln_in, 16)
                else:
                    dve.wait_ge(s_xs[b % 2], 16 * ((B - b - 1) // 2 + 1))
                if i >= 2:
                    dve.wait_ge(s_aggr, i - 1)
                nc.vector.bn_stats(stats1[:, i % 2, :], (x_hat if b % 2 else x_ln)[:, t, :]).then_inc(s_stat, 1)
                dve.wait_ge(s_stat, i + 1)
                nc.vector.bn_aggr(mv1[:, NT * b + t, :], stats1[:, i % 2, :]).then_inc(s_aggr, 1)

            def to_float(i):
                name, raw = (("wg", wg_raw), ("wu", wu_raw), ("wd", wd_raw))[i]
                dve.wait_ge(s_in[name], 16)
                nc.vector.tensor_copy(raw[:], raw[:].bitcast(I32)).then_inc(s_float, 1)

            stats_at = 0
            for n in dve_jobs:
                if n < first_v:
                    copy(n)
                if first_t <= n < first_v:
                    for _ in range(STATS_PER_JOB):
                        if stats_at < B * NT:
                            stat(stats_at)
                            stats_at += 1
                if n == first_t - 1:
                    dve.wait_ge(s_tgate, 1)
                    nc.vector.tensor_scalar(bias[:], bias[:], tgate[:, 0:1], None, ALU.mult).then_inc(s_bias, 1)

            def maxima(b, u):
                dve.wait_ge(scores_done, NU * b + u + 1)
                s = ps_s[:, u % 2, :, 0:BK].rearrange("p r (h k) -> p r h k", k=K)
                if not (isinstance(b, int) and b == 0):
                    dve.wait_ge(sub_done, NU * (b - 1) + u + 1)
                nc.vector.reduce_max(top[:, u, :].rearrange("p (r h) -> p r h", r=2), s, AXIS_X).then_inc(max_done, 1)
                dve.wait_ge(max_done, NU * b + u + 1)
                if not (isinstance(b, int) and b == 0):
                    dve.wait_ge(pt_done, 8 * (b - 1) + 2 * (u + 1))
                nc.vector.tensor_tensor(
                    probs[:, u, :].rearrange("p (r h k) -> p r h k", r=2, k=K), s,
                    top[:, u, :].rearrange("p (r h) -> p r h", r=2).unsqueeze(3).to_broadcast([P, 2, HB, K]),
                    ALU.subtract).then_inc(sub_done, 1)

            def sums(b, u):
                dve.wait_ge(exp_done, NU * b + u + 1)
                if not (isinstance(b, int) and b == 0):
                    dve.wait_ge(probs_done, NU * (b - 1) + u + 1)
                nc.vector.reduce_sum(total[:, u, :], probs[:, u, :].rearrange("p (h k) -> p h k", k=K),
                                     AXIS_X).then_inc(sum_done, 1)
                dve.wait_ge(sum_done, NU * b + u + 1)
                nc.vector.reciprocal(total[:, u, :], total[:, u, :]).then_inc(rec_done, 1)

            def split_o(b, g):
                for i in range(2):
                    n = 2 * g + i
                    dve.wait_ge(ohi_done, NU * b + n + 1)
                    if n == 0:
                        wait(dve, proj_done, NT * b)
                        if isinstance(b, int) and b == 0:
                            dve.wait_ge(s_wol, 1)
                    nc.vector.tensor_tensor(o_lo[:, 2 * n:2 * n + 2, :],
                                            ps_p[:, i, :].rearrange("p (i q) -> p i q", i=2),
                                            o_hi[:, 2 * n:2 * n + 2, :].bitcast(F32), ALU.subtract).then_inc(olo_done, 1)

            def split_x2(b):
                dve.wait_ge(x2hi_done, b)
                nc.vector.tensor_tensor(x2_lo[:], ps_m[:, bank["X1T"], :].rearrange("p (c q) -> p c q", c=DC),
                                        x2_hi[:].bitcast(F32), ALU.subtract).then_inc(x2lo_done, 1)

            def hidden(b, f):
                n = FC * (b - 1) + f
                dve.wait_ge(tanh_done, n + 1)
                if f >= 2:
                    dve.wait_ge(hlo_done, n - 1)
                nc.vector.scalar_tensor_tensor(hid[:, f % 2, :], tanh_g[:, f % 2, :], 1.0,
                                               ps_m[:, bank[f"G{f}"], 0:Q], ALU.add, ALU.mult).then_inc(gated, 1)
                dve.wait_ge(gated, n + 1)
                nc.vector.tensor_tensor(hid[:, f % 2, :], hid[:, f % 2, :], ps_m[:, bank[f"G{f}"], Q:2 * Q],
                                        ALU.mult).then_inc(hid_done, 1)

            def normalise_x(n):
                if isinstance(n, int) and n == 0:
                    dve.wait_ge(s_ln, X_STEPS)
                dve.wait_ge(xln_in, 16 * (n + 1))
                if not (isinstance(n, int) and n == 0):
                    dve.wait_ge(xt_done, n)
                for t in range(NT):
                    col = NT * n + t
                    at = slice(col, col + 1) if isinstance(n, int) else bass.ds(col, 1)
                    nc.vector.tensor_scalar(x_hat[:, t, :], x_ln[:, t, :], mean1[:, at], rstd1[:, at],
                                            ALU.subtract, ALU.mult).then_inc(xhat_done, 1)

            def result(b, t):
                dve.wait_ge(down_done, NT * (b - 1) + t + 1)
                nc.vector.scalar_tensor_tensor(x1[:, t, :], ps_m[:, bank[f"D{t}"], 0:D], 0.5 * QUANT ** 3,
                                               x1[:, t, :], ALU.mult, ALU.add).then_inc(y_done, 1)

            def residual(b, t):
                dve.wait_ge(proj_done, NT * b + t + 1)
                if t == 0:
                    dve.wait_ge(xres_biased, b + 1)
                    wait(dve, y_out, 16 * b)
                nc.vector.scalar_tensor_tensor(x1[:, t, :], ps_m[:, bank[f"O{t}"], 0:D], tgate[:, 0:1], x_res[:, t, :],
                                               ALU.mult, ALU.add).then_inc(x1_done, 1)
                dve.wait_ge(x1_done, NT * b + t + 1)
                nc.vector.bn_stats(stats[:, t, :], x1[:, t, :]).then_inc(stat_done, 1)

            def aggregate(b):
                dve.wait_ge(stat_done, NT * (b + 1))
                nc.vector.memset(spare[:], 0.0).then_inc(spare_cleared, 1)
                for t in range(NT):
                    nc.vector.bn_aggr(mv[:, t, :], stats[:, t, :]).then_inc(aggr_done, 1)
                if isinstance(b, int) and b == B - 1:
                    last_norm_scale()

            def last_norm_scale():
                dve.wait_ge(aggr_done, NT * B)
                done = [LN_STEPS * (B - 1)]

                def step(ins, signals=1):
                    done[0] += signals
                    ins.then_inc(ln_step, signals)
                    if done[0] < LN_STEPS * B:
                        dve.wait_ge(ln_step, done[0])

                step(nc.vector.tensor_scalar(var_eps[:], mv[:, :, 1], EPS, None, ALU.add))
                step(nc.vector.tensor_scalar(rstd[:].bitcast(I32), var_eps[:].bitcast(I32), -0.5, RSQRT_SEED,
                                             ALU.mult, ALU.add))
                for i in range(3):
                    step(nc.vector.tensor_tensor(tmp[:], rstd[:], rstd[:], ALU.mult))
                    step(nc.vector.scalar_tensor_tensor(tmp[:], tmp[:], -0.5, var_eps[:], ALU.mult, ALU.mult))
                    step(nc.vector.scalar_tensor_tensor(rstd[:], tmp[:], 1.5, rstd[:], ALU.add, ALU.mult),
                         LN_STEPS - 10 if i == 2 else 1)

            def normalise_x1(b):
                dve.wait_ge(ln_step, LN_STEPS * (b + 1))
                for t in range(NT):
                    nc.vector.tensor_scalar(x1_hat[:, t, :], x1[:, t, :], mv[:, t, 0:1], rstd[:, t:t + 1],
                                            ALU.subtract, ALU.mult).then_inc(x1hat_done, 1)

            stages = {"X1": ("ffn", split_x2), "LN": ("next", normalise_x), "AG": ("now", aggregate),
                      "LN1": ("ffn", lambda b: normalise_x1(b - 1))}
            for u in range(NU):
                stages[f"M{u}"] = ("next" if u < HOISTED else "now", maxima, u)
                stages[f"Z{u}"] = ("next" if u < HOISTED else "now", sums, u)
            for t in range(NT):
                stages[f"O{t}"] = ("now", split_o, t)
                stages[f"Y{t}"] = ("ffn", result, t)
                stages[f"R{t}"] = ("now", residual, t)
            for f in range(FC):
                stages[f"H{f}"] = ("ffn", hidden, f)
            for i in range(3):
                stages[f"F{i}"] = ("start", to_float, i)
            stages["job"] = copy
            batches(dve, DVE_START, DVE_ORDER, stages)


_INS = ["x", "ctx_1024", "L0_xattn_ln_gamma", "L0_xattn_ln_beta", "L0_xattn_w_q", "L0_xattn_w_kv",
        "L0_xattn_w_out", "L0_xattn_b_out", "L0_xattn_gate", "L0_ffn_w_gate", "L0_ffn_w_up", "L0_ffn_w_down"]


def kernel(**inputs):
    import numpy as np
    import concourse.bacc as bacc
    from concourse.bass_utils import run_bass_kernel_spmd

    nc = bacc.Bacc("TRN2", target_bir_lowering=False, num_devices=1)
    arrays, args = {}, []
    for name in _INS:
        a = np.ascontiguousarray(inputs[name])
        arrays[f"in_{name}"] = a
        args.append(nc.dram_tensor(f"in_{name}", a.shape, mybir.dt.from_np(a.dtype), kind="ExternalInput").ap())
    shape = arrays["in_x"].shape
    args.append(nc.dram_tensor("out", shape, F32, kind="ExternalOutput").ap())
    xattn_ffn_kernel(nc, *args)
    r = run_bass_kernel_spmd(nc, [arrays], core_ids=[0])
    return r.results[0]["out"]
```

```python
from contextlib import ExitStack

import concourse.bass as bass
from concourse import mybir

F32 = mybir.dt.float32
F32R = mybir.dt.float32r
I32 = mybir.dt.int32
ACT = mybir.ActivationFunctionType
ALU = mybir.AluOpType
AXIS_X = mybir.AxisListType.X

P = 128
BANK = 512
HEADS = 16
EPS = 1e-5
RSQRT_SEED = 0x5F3759DF
HOISTED = 2

PE_ORDER = "S2 S3 T0 T1 X1T XT V0 G0 G1 T2 G2 G3 T3 G4 V1 G5 S0 S1 O0 O1 D0 D1".split()
DVE_ORDER = "M2 M3 LN1 Z2 LN X1 Z3 O0 H0 H1 H2 H3 H4 O1 H5 M0 Z0 R0 M1 R1 AG Y0 Y1 Z1".split()
ACT_ORDER = "Ta E2 C0 C1 X1 E3 X O0 t0 t1 h0 C2 t2 h1 t3 C3 h2 h3 t4 O1 Tb t5 h4 E0 h5 E1".split()
POOL_ORDER = "P2 B X P3 h0 h1 Ta h2 h3 h4 h5 Tb P0 LN P1".split()
SP_ORDER = "RES LN V OUT".split()
PE_START = "v0 v2 v1 XT v3 v4 v5 FL S0 v6 S1 v7 v8 v9".split()
ACT_START = "Ta X v3 v2 v1 v5 v4 Tb v6 E0 E1 WO".split()
DVE_START = "F0 LN v0 F2 B0 F1 B2 B1 BC BR M0 M1 Z0 v7 v8 v9 Z1".split()
POOL_START = "XS Ta X Tb P0 P1 WO".split()
ACT_TS = "1 3 4 6 7".split()
WARM_UP = (8, 12, 18, 6)
STATS_PER_JOB = 2
EXACT = 4096.0
QUANT = 1.0 / 127.0


def xattn_ffn_kernel(nc, x, ctx_in, ln_gamma, ln_beta, w_q, w_kv, w_out, b_out, gate,
                     w_gate, w_up, w_down, out):
    B, S, D = x.shape
    K = ctx_in.shape[1]
    INNER = w_q.shape[1]
    DH = INNER // HEADS
    HID = w_gate.shape[0]
    DC = D // P
    NT = S // P
    IC = INNER // P
    FC = HID // P
    HK = HEADS * K
    HG = HEADS // 2
    HB = HG // 2
    CR = B * K
    RC = (CR + P - 1) // P
    HALF = B // 2
    HC = HALF * K
    SCALE = DH ** -0.5
    NU = 2 * NT
    GK = HG * K
    BK = HB * K
    Q = NT * P
    WP = 4
    VS = 4
    LN_STEPS = 3 + 12
    X_STEPS = 4 + 12
    assert HB * K <= BANK and DC == 2 and NT == 2 and 2 * DH == P and RC == VS + 1 and K <= P

    x_dram = x.rearrange("b (t p) d -> p b t d", p=P)
    out_dram = out.rearrange("b (t p) d -> p b t d", p=P)
    ctx_rows = ctx_in.rearrange("b k d -> (b k) d")
    v_scratch = nc.dram_tensor("v_scratch", (CR, INNER), F32, kind="Internal").ap()

    whole, weights_in, parts_in, before_loop = ExitStack(), ExitStack(), ExitStack(), ExitStack()
    with whole:
        def sem(name):
            return whole.enter_context(nc.semaphore(name))

        def sb(name, shape, dt=F32, where=whole):
            return where.enter_context(nc.sbuf_tensor(name, shape, dt))

        wo_hi = sb("wo_hi", [P, IC, D], F32R)
        wo_lo = sb("wo_lo", [P, IC, D], F32R)
        wv_hi = wo_hi[:].rearrange("p i d -> p (i d)").rearrange("p (c n) -> p c n", c=DC)
        wv_lo = wo_lo[:].rearrange("p i d -> p (i d)").rearrange("p (c n) -> p c n", c=DC)
        ident = sb("ident", [P, P])
        gamma = sb("gamma", [P, DC])
        beta = sb("beta", [P, DC])
        tgate = sb("tgate", [P, 1])
        bias = sb("bias", [P, D])
        consts = sb("consts", [P, 3, B * NT])
        mean1 = sb("mean1", [P, B * NT])
        rstd1 = sb("rstd1", [P, B * NT])
        largest = sb("largest", [P, 3])
        largest_row = sb("largest_row", [P, 1])
        largest_of_all = sb("largest_of_all", [1, 1])
        inexact = sb("inexact", [1, 1], I32)
        x_ln = sb("x_ln", [P, NT, D])
        x_hat = sb("x_hat", [P, NT, D])

        with weights_in:
            wv_raw = sb("wv_raw", [P, DC, INNER], where=weights_in)
            wqt_own = sb("wqt_own", [P, IC, D], F32R, where=weights_in)
            stats1 = sb("stats1", [P, 2, 6], where=weights_in)
            mv1 = sb("mv1", [P, B * NT, 2], where=weights_in)
            var1 = sb("var1", [P, B * NT], where=weights_in)
            half1 = sb("half1", [P, B * NT], where=weights_in)
            tmp1 = sb("tmp1", [P, B * NT], where=weights_in)
        wg = sb("wg", [P, DC, HID], F32R)
        wu = sb("wu", [P, DC, HID], F32R)
        wd = sb("wd", [P, FC, D], F32R)

        with parts_in:
            ctx_raw = sb("ctx_raw", [P, RC, D], where=parts_in)
            wk_raw = sb("wk_raw", [P, DC, INNER], where=parts_in)
            wk_hi = sb("wk_hi", [P, DC, INNER], F32R, where=parts_in)
            wk_lo = sb("wk_lo", [P, DC, INNER], F32R, where=parts_in)
            wq_raw = sb("wq_raw", [P, DC, INNER], where=parts_in)
        t_all = sb("t_all", [P, DC, B, HK])

        with before_loop:
            wqt_hi = sb("wqt_hi", [P, IC, 2, D], F32R, where=before_loop)
            wqt_lo = sb("wqt_lo", [P, IC, D], F32R, where=before_loop)
            kt = sb("kt", [P, HEADS, CR], F32R, where=before_loop)
            sb("gap", [P, 160], where=before_loop)
            wg_raw = sb("wg_raw", [P, FC, D], where=before_loop)
            wu_raw = sb("wu_raw", [P, FC, D], where=before_loop)
            wd_raw = sb("wd_raw", [P, DC, HID], where=before_loop)
            ct_hi = sb("ct_hi", [P, DC, CR], F32R, where=before_loop)
            ct_lo = sb("ct_lo", [P, DC, CR], F32R, where=before_loop)

        t_hi = sb("t_hi", [P, DC, HK], F32R)
        t_lo = sb("t_lo", [P, DC, HK], F32R)
        xn = sb("xn", [P, DC, Q])
        xn_hi = sb("xn_hi", [P, DC, Q], F32R)
        xn_lo = sb("xn_lo", [P, DC, Q], F32R)
        probs = sb("probs", [P, NU, GK])
        top = sb("top", [P, NU, HG])
        total = sb("total", [P, NU, HG])
        v = sb("v", [K, INNER])
        with ExitStack() as after_t:
            v_out = sb("v_out", [P, VS, INNER], where=after_t)
            wo_raw = sb("wo_raw", [P, IC, D], where=after_t)
        pt = sb("pt", [K, HG, Q])
        o_hi = sb("o_hi", [P, IC, Q], F32R)
        o_lo = sb("o_lo", [P, IC, Q], F32R)
        with ExitStack() as raw_read:
            wu_t = sb("wu_t", [P, DC, HID], where=raw_read)
            wd_t = sb("wd_t", [P, FC, D], where=raw_read)
        h_hi = sb("h_hi", [P, FC, Q], F32R)
        h_lo = sb("h_lo", [P, FC, Q], F32R)
        x1_hat = sb("x1_hat", [P, NT, D])
        x2_hi = sb("x2_hi", [P, DC, Q], F32R)
        x2_lo = sb("x2_lo", [P, DC, Q], F32R)
        with ExitStack() as v_made:
            sb("slot", [P, NT, D], where=v_made)
            wg_t = sb("wg_t", [P, DC, HID], where=v_made)
        stream = sb("stream", [P, 2, NT, D])
        tanh_g = sb("tanh_g", [P, 2, Q])
        hid = sb("hid", [P, 2, Q])
        stats = sb("stats", [P, NT, 6])
        mv = sb("mv", [P, NT, 2])
        var_eps = sb("var_eps", [P, NT])
        half_var = sb("half_var", [P, NT])
        rstd = sb("rstd", [P, NT])
        tmp = sb("tmp", [P, NT])
        spare = sb("spare", [P, 1])
        spare_pool = sb("spare_pool", [P, NT])

        ps = whole.enter_context(nc.psum_tensor("ps", [P, 8, BANK], F32))
        ps_s = ps[:, 0:4, :].rearrange("p (u r) n -> p u r n", u=2)
        ps_p = ps[:, 4:6, :]
        ps_m = ps[:, 6:8, :]

        s_in = {n: sem(f"in_{n}") for n in "ctx wq wv wo wg wu wd small".split()}
        s_wk = [sem(f"in_wk_{i}") for i in range(WP)]
        s_xs = [sem(f"x_for_stats_{i}") for i in range(2)]
        s_dup = [sem(f"wq_hi_doubled_{i}") for i in range(2)]
        s_vfirst, s_vrest = sem("v_first_rows_stored"), sem("v_other_rows_stored")
        s_ident0, s_ident = sem("ident_zeroed"), sem("ident_ready")
        s_job = sem("job_done")
        s_act, s_dve = sem("job_copied_by_act"), sem("job_copied_by_dve")
        s_wkh, s_wkl = sem("wk_hi_ready"), sem("wk_lo_ready")
        s_wvh, s_wvl = sem("wv_hi_ready"), sem("wv_lo_ready")
        s_woh, s_wol = sem("wo_hi_ready"), sem("wo_lo_ready")
        s_float = [sem(f"{n}_made_float") for n in ("wg", "wu", "wd")]
        s_large = [sem(f"largest_of_{n}") for n in ("wg", "wu", "wd")]
        s_row, s_rows = sem("largest_of_a_partition"), sem("largest_of_partitions_transposed")
        s_flag = sem("inexact_flag_step")
        s_wf = [sem(f"{n}_in_place") for n in ("wg", "wu", "wd")]
        s_tgate, s_bias = sem("tanh_gate_ready"), sem("bias_ready")
        s_stat, s_aggr, s_ln = sem("x_stats_done"), sem("x_aggr_done"), sem("x_norm_step")
        xln_in, xres_in, v_in, y_out = sem("xln_in"), sem("xres_in"), sem("v_in"), sem("y_out")
        scores_done, pt_done, pv_done = sem("scores_done"), sem("pt_done"), sem("pv_done")
        xt_done, x2t_done, gu_done = sem("xt_done"), sem("x2t_done"), sem("gu_done")
        down_done, proj_done = sem("down_done"), sem("proj_done")
        max_done, sub_done, sum_done, rec_done = sem("max_done"), sem("sub_done"), sem("sum_done"), sem("rec_done")
        olo_done, x2lo_done, gated, hid_done = sem("olo_done"), sem("x2lo_done"), sem("gated"), sem("hid_done")
        x1_done, stat_done, ln_step, x1hat_done = sem("x1_done"), sem("stat_done"), sem("ln_step"), sem("x1hat_done")
        aggr_done, spare_cleared = sem("aggr_done"), sem("spare_cleared")
        consts_set = sem("consts_set")
        xhat_done, y_done = sem("xhat_done"), sem("y_done")
        exp_done, pt_copied, ohi_done = sem("exp_done"), sem("pt_copied"), sem("ohi_done")
        thi_done, tanh_done, hhi_done = sem("thi_done"), sem("tanh_done"), sem("hhi_done")
        x2hi_done, xn_done, xnhi_done = sem("x2hi_done"), sem("xn_done"), sem("xnhi_done")
        probs_done, tlo_done, hlo_done = sem("probs_done"), sem("tlo_done"), sem("hlo_done")
        xres_biased, xnlo_done = sem("xres_biased"), sem("xnlo_done")

        shared = [n for n in PE_ORDER if n in ("X1T", "XT", "G0", "G1", "G2", "G3", "G4", "G5", "D0", "D1", "O0", "O1")]
        bank = {n: i % 2 for i, n in enumerate(shared)}

        def last_user(b, name):
            at = shared.index(name) - 2
            while at >= 0:
                n, k = shared[at], int(shared[at][1]) if shared[at][1].isdigit() else 0
                if n == "XT" and not (isinstance(b, int) and b >= B - 1):
                    return xn_done, DC * (b + 2)
                if n[0] == "O" and not (isinstance(b, int) and b == B):
                    return x1_done, NT * b + k + 1
                if isinstance(b, int) and b == 0 and n in stand_in:
                    return s_dve, by_dve[stand_in[n]]
                if not (isinstance(b, int) and b == 0):
                    if n == "X1T":
                        return x2lo_done, b
                    if n[0] == "G":
                        return hid_done, FC * (b - 1) + k + 1
                    if n[0] == "D":
                        return y_done, NT * (b - 1) + k + 1
                at -= 2
            return None

        def wait(eng, s, value):
            if isinstance(value, int) and value <= 0:
                return
            eng.wait_ge(s, value)

        jobs = [("ctx", r) for r in range(RC)]
        for step in "k0 k1 k2 w0 w1 k3 k4 w2 w3 k5 k6 k7".split():
            jobs += [("k" if step[0] == "k" else "wq", int(step[1:]))]
        jobs += [("t", h, n) for h in range(HEADS) for n in range(2)]
        first_t, last_t = jobs.index(("t", 0, 0)), len(jobs) - 1
        first_v = len(jobs)
        jobs += [("v", r, n) for r in range(RC) for n in range(2)]
        last_v = len(jobs) - 1
        first_f = len(jobs)
        stand_in = {n: first_f + i for i, n in enumerate(m for m in PE_ORDER if m == "X1T" or m[0] in "GD")}
        copied_at = {"X1" if n == "X1T" else ("H" if n[0] == "G" else "Y") + n[1]: m for n, m in stand_in.items()}
        jobs += [(w, f) for w in ("wg", "wu", "wd") for f in range(FC // 2)]
        other = 6 + 1 - bank["XT"]

        def banks_of(n):
            j = jobs[n]
            if j[0] == "ctx":
                return [j[1]]
            if j[0] == "k":
                at = 2 * ((j[1] + 1) % 3)
                return [at, at + 1]
            if j[0] == "wq":
                return [6 + j[1] % 2]
            if j[0] == "t":
                at = 2 * ((n - first_t) % 4)
                return [at, at + 1]
            if j[0] == "v":
                return [(4, 5, other)[(n - first_v) % 3]]
            return [6 + bank[{m: n for n, m in stand_in.items()}[n]]]

        def job_of(token):
            if token[0] == "v":
                return first_v + int(token[1:])

        act_t = {first_t + i for i in range(2 * HEADS) if str(i % 8) in ACT_TS}
        both = [n for n in range(first_t)]
        act_jobs = both + sorted(act_t) + [job_of(s) for s in ACT_START if job_of(s) is not None]
        dve_jobs = both + [n for n in range(first_t, first_v) if n not in act_t]
        dve_jobs += [job_of(s) for s in DVE_START if job_of(s) is not None]
        dve_jobs += [copied_at[s] for s in DVE_ORDER if s in copied_at]
        by_act = {n: i + 1 for i, n in enumerate(act_jobs)}
        by_dve = {n: i + 1 for i, n in enumerate(dve_jobs)}
        holder, before = {}, []
        for n in range(len(jobs)):
            before.append(sorted({holder[k] for k in banks_of(n) if k in holder}))
            holder.update({k: n for k in banks_of(n)})

        def evacuated(eng, n):
            if n in by_act:
                eng.wait_ge(s_act, by_act[n])
            if n in by_dve:
                eng.wait_ge(s_dve, by_dve[n])

        turn_parity = [0]

        def residual_of(b, ago=0):
            return stream[:, (turn_parity[0] + ago) % 2]

        def last(b):
            return isinstance(b, int) and b == B

        def gate_up_psum(b, f):
            return ps[:, f, :] if last(b) else ps_m[:, bank[f"G{f}"], :]

        def rows(r):
            return min(P, CR - r * P)

        def psum_of(n):
            j, b = jobs[n], banks_of(n)[0]
            if j[0] == "ctx":
                return ps[:, b, 0:DC * P].rearrange("p (c r) -> p c r", c=DC)[:, :, 0:rows(j[1])]
            if j[0] == "v":
                return ps[0:rows(j[1]), b, :]
            if j[0] == "k":
                return ps[:, b:b + 2, 0:HC]
            if j[0] == "t":
                return ps[:, b:b + 2, 0:HC].rearrange("p c (b k) -> p c b k", k=K)
            return ps[:, b, :].rearrange("p (c r) -> p c r", c=2)

        def target(n):
            j = jobs[n]
            if j[0] == "v":
                return v_out[0:rows(j[1]), j[1] % VS, j[2] * BANK:(j[2] + 1) * BANK]
            if j[0] == "wg":
                return wg_t[:, :, j[1] * 2 * P:(j[1] + 1) * 2 * P]
            if j[0] == "wu":
                return wu_t[:, :, j[1] * 2 * P:(j[1] + 1) * 2 * P]
            if j[0] == "wd":
                return wd_t[:, 2 * j[1]:2 * j[1] + 2, :]
            return t_all[:, :, j[2] * HALF:(j[2] + 1) * HALF, j[1] * K:(j[1] + 1) * K]

        def parts(n):
            j = jobs[n]
            if j[0] == "ctx":
                cols = slice(j[1] * P, j[1] * P + rows(j[1]))
                return [(psum_of(n), ct_hi[:, :, cols], ct_lo[:, :, cols])]
            halves = [slice(0, DH), slice(DH, P)]
            if j[0] == "k":
                return [(psum_of(n)[halves[e]], kt[halves[e], 2 * j[1] + e, :].rearrange("p (n c) -> p n c", n=2),
                         kt[halves[1 - e], 2 * j[1] + e, :].rearrange("p (n c) -> p n c", n=2)) for e in range(2)]
            pairs = slice(2 * j[1], 2 * j[1] + 2)
            return [(psum_of(n), wqt_own[:, pairs, :], wqt_lo[:, pairs, :])]

        def rsqrt(step, carry, r, v, half, tmp):
            tt = nc.gpsimd.tensor_tensor
            n = v.shape[1]
            step(tt(half, v, consts[:, 1, 0:n], ALU.mult))
            carry()
            step(nc.gpsimd.tensor_scalar(r.bitcast(I32), v.bitcast(I32), -0.5, RSQRT_SEED, ALU.mult, ALU.add))
            for _ in range(3):
                step(tt(tmp, r, r, ALU.mult))
                step(tt(tmp, tmp, half, ALU.mult))
                step(tt(tmp, tmp, consts[:, 2, 0:n], ALU.add))
                step(tt(r, tmp, r, ALU.mult))

        def start(order, stages):
            for name in order:
                part, fn, *args = stages.get(name, (None, None))
                if part == "start":
                    fn(*args)
                elif part == "next":
                    fn(0, *args)
                else:
                    stages["job"](job_of(name))

        def batches(eng, order, stages):
            def body(b, now=True, ffn=True, nxt=True, parity=1):
                turn_parity[0] = b % 2 if isinstance(b, int) else parity
                for name in order:
                    part, fn, *args = stages[name]
                    if part == "now" and now:
                        fn(b, *args)
                    if part == "ffn" and ffn:
                        fn(b, *args)
                    if part == "ffn" and not ffn and "fill" in stages:
                        stages["fill"](name)
                    if part == "next" and nxt:
                        fn(b + 1, *args)

            body(0, ffn=False)
            with eng.Fori(0, (B - 2) // 2) as pair:
                body(2 * pair + 1)
                body(2 * pair + 2, parity=0)
            body(B - 1, nxt=False)
            body(B, now=False, nxt=False)

        block = whole.enter_context(nc.Block())

        @block.sync
        def _(sp):
            def weights_in_place(i):
                for f in range(FC // 2):
                    evacuated(sp, first_f + i * FC // 2 + f)
                sp.dma_start((wg, wu, wd)[i][:].bitcast(F32), (wg_t, wu_t, wd_t)[i][:]).then_inc(s_wf[i], 16)

            def load_res(b):
                if isinstance(b, int) and b == 0:
                    sp.wait_ge(s_job, last_v + 1)
                if isinstance(b, int) and b == 1:
                    sp.wait_ge(s_wf[0], 16)
                if not (isinstance(b, int) and b < 2):
                    sp.wait_ge(y_out, 16 * (b - 1))
                sp.dma_start(residual_of(b), x_dram[:, b]).then_inc(xres_in, 16)

            def load_ln(n):
                wait(sp, xhat_done, NT * n)
                sp.dma_start(x_ln[:], x_dram[:, n]).then_inc(xln_in, 16)

            def store(b):
                sp.wait_ge(y_done, NT * b)
                sp.dma_start(out_dram[:, b - 1], residual_of(b, 1)).then_inc(y_out, 16)

            def load_v(n):
                if isinstance(n, int) and n == 1:
                    weights_in_place(0)
                    weights_in_place(1)
                    sp.wait_ge(s_vrest, 16 * (RC - 1))
                wait(sp, pv_done, NU * n)
                sp.dma_start(v[:], v_scratch.rearrange("(b k) n -> b k n", k=K)[n]).then_inc(v_in, 16)
                if isinstance(n, int) and n == 1:
                    weights_in_place(2)

            sp.dma_start(ctx_raw[:, 0:RC - 1, :],
                         ctx_rows[0:(RC - 1) * P, :].rearrange("(r p) d -> p r d", p=P)).then_inc(s_in["ctx"], 16)
            sp.dma_start(ctx_raw[0:rows(RC - 1), RC - 1, :], ctx_rows[(RC - 1) * P:CR, :]).then_inc(s_in["ctx"], 16)
            w_kv_rows = w_kv.rearrange("(c p) n -> p c n", p=P)
            for i in range(WP):
                cols = slice(i * INNER // WP, (i + 1) * INNER // WP)
                sp.dma_start(wk_raw[:, :, cols], w_kv_rows[:, :, cols]).then_inc(s_wk[i], 16)
                if i == 0:
                    sp.dma_start(wq_raw[:], w_q.rearrange("(c p) n -> p c n", p=P)).then_inc(s_in["wq"], 16)
            sp.dma_start(wv_raw[:], w_kv_rows[:, :, INNER:2 * INNER]).then_inc(s_in["wv"], 16)
            for name, raw, w in (("wg", wg_raw, w_gate), ("wu", wu_raw, w_up), ("wd", wd_raw, w_down)):
                sp.dma_start(raw[:].bitcast(I32), w.rearrange("(r p) n -> p r n", p=P)).then_inc(s_in[name], 16)
            for b in range(B - 1, -1, -1):
                if b == B - 3:
                    for i in range(2):
                        sp.wait_ge(s_act, by_act[jobs.index(("wq", 2 * i + 1))])
                        pairs = slice(4 * i, 4 * i + 4)
                        for e in range(2):
                            for to in range(2):
                                sp.dma_start(wqt_hi[to * DH:(to + 1) * DH, pairs, e, :].bitcast(F32),
                                             wqt_own[e * DH:(e + 1) * DH, pairs, :].bitcast(F32)).then_inc(s_dup[i], 16)
                if b < B - 2:
                    sp.wait_ge(s_stat, NT * (B - 2 - b))
                sp.dma_start((x_hat if b % 2 else x_ln)[:], x_dram[:, b]).then_inc(xln_in if b == 0 else s_xs[b % 2], 16)
            sp.wait_ge(s_job, last_t + 1)
            sp.dma_start(wo_raw[:], w_out.rearrange("(i p) n -> p i n", p=P)).then_inc(s_in["wo"], 16)
            for r in range(RC):
                for n in range(2):
                    evacuated(sp, first_v + 2 * r + n)
                sp.dma_start(v_scratch[r * P:r * P + rows(r), :],
                             v_out[0:rows(r), r % VS, :]).then_inc(s_vfirst if r == 0 else s_vrest, 16)
                if r == 1:
                    sp.wait_ge(s_vfirst, 16)
                    load_v(0)

            batches(sp, SP_ORDER, {"RES": ("now", load_res), "LN": ("next", load_ln),
                                   "OUT": ("ffn", store), "V": ("next", load_v)})
            sp.wait_ge(y_out, 16 * B)

        @block.tensor
        def _(pe):
            mm = nc.tensor.matmul

            def job(n):
                j = jobs[n]
                kind = j[0]
                for m in before[n]:
                    evacuated(pe, m)
                if n >= first_f:
                    claim(0, {m: s for s, m in stand_in.items()}[n])
                    pe.wait_ge(xn_done, DC)
                o = psum_of(n)
                if kind == "ctx":
                    m = rows(j[1])
                    for c in range(DC):
                        ins = nc.tensor.transpose(o[:, c, :], ctx_raw[0:m, j[1], c * P:(c + 1) * P], ident[0:m, 0:m])
                if kind == "k":
                    i = j[1]
                    if i == 0:
                        evacuated(pe, RC - 1)
                    if i % (IC // WP) == 0:
                        pe.wait_ge(s_wkl, i // (IC // WP) + 1)
                    ws = slice(i * P, (i + 1) * P)
                    for n2 in range(2):
                        cols = slice(n2 * HC, (n2 + 1) * HC)
                        for c in range(DC):
                            mm(o[:, n2, :], wk_hi[:, c, ws], ct_hi[:, c, cols], start=c == 0, stop=False)
                            mm(o[:, n2, :], wk_hi[:, c, ws], ct_lo[:, c, cols], start=False, stop=False)
                            ins = mm(o[:, n2, :], wk_lo[:, c, ws], ct_hi[:, c, cols], start=False, stop=c == DC - 1)
                if kind == "wq":
                    if j[1] == 0:
                        pe.wait_ge(s_in["wq"], 16)
                    for a in range(2):
                        i = 2 * j[1] + a
                        for c in range(DC):
                            ins = nc.tensor.transpose(o[:, a, c * P:(c + 1) * P],
                                                      wq_raw[:, c, i * P:(i + 1) * P], ident[:])
                if kind == "t":
                    h, half = j[1:]
                    if half == 0:
                        evacuated(pe, jobs.index(("k", h // 2)))
                        evacuated(pe, jobs.index(("wq", h // 4)))
                        pe.wait_ge(s_dup[h // 8], 64)
                    i, ds = h // 2, slice((h % 2) * DH, (h % 2 + 1) * DH)
                    cols = slice(half * HC, (half + 1) * HC)
                    for c in range(DC):
                        oc = ps[:, banks_of(n)[c], 0:HC]
                        ws = slice(c * P, (c + 1) * P)
                        mm(oc, wqt_hi[:, i, h % 2, ws], kt[:, h, cols], start=True, stop=False)
                        ins = mm(oc, wqt_lo[ds, i, ws], kt[ds, h, cols], start=False, stop=True)
                if kind == "v":
                    if n == first_v:
                        pe.wait_ge(s_wvl, 1)
                    cols = slice(j[2] * BANK, (j[2] + 1) * BANK)
                    rs = slice(j[1] * P, j[1] * P + rows(j[1]))
                    for c in range(DC):
                        mm(o, ct_hi[:, c, rs], wv_hi[:, c, cols], start=c == 0, stop=False)
                        mm(o, ct_hi[:, c, rs], wv_lo[:, c, cols], start=False, stop=False)
                        ins = mm(o, ct_lo[:, c, rs], wv_hi[:, c, cols], start=False, stop=c == DC - 1)
                if kind in ("wg", "wu", "wd"):
                    if j[1] == 0:
                        which = ("wg", "wu", "wd").index(kind)
                        pe.wait_ge(s_float[which], 1)
                        if which > 0:
                            pe.wait_ge(s_large[which - 1], 1)
                    for a in range(2):
                        for c in range(2):
                            if kind == "wd":
                                f = 2 * j[1] + a
                                ins = nc.tensor.transpose(o[:, a, c * P:(c + 1) * P],
                                                          wd_raw[:, c, f * P:(f + 1) * P], ident[:])
                            else:
                                raw = wg_raw if kind == "wg" else wu_raw
                                ins = nc.tensor.transpose(o[:, c, a * P:(a + 1) * P],
                                                          raw[:, 2 * j[1] + a, c * P:(c + 1) * P], ident[:])
                ins.then_inc(s_job, 1)

            def warm_up(at, times):
                for _ in range(times):
                    mm(ps[:, at, 0:P], ident[:], ident[:], start=True, stop=True)

            def transpose_largest():
                pe.wait_ge(s_row, 1)
                evacuated(pe, last_t - 2)
                nc.tensor.transpose(ps[0:1, 3, 0:P], largest_row[:], ident[:]).then_inc(s_rows, 1)

            pe.wait_ge(s_ident, 1)
            warm_up(7, WARM_UP[0])
            pe.wait_ge(s_in["ctx"], 32)
            for n in range(first_v):
                job(n)
                if n == RC - 1:
                    warm_up(7, WARM_UP[1])

            def claim(b, name):
                if isinstance(b, int) and b < 0:
                    return
                user = last_user(b, name)
                if user:
                    pe.wait_ge(*user)

            def scores(b, u):
                g, t = divmod(u, NT)
                if u == 0:
                    pe.wait_ge(xnhi_done, b + 1)
                    pe.wait_ge(xnlo_done, b + 1)
                if t == 0:
                    pe.wait_ge(tlo_done, 2 * b + g + 1)
                wait(pe, sub_done, NU * b + u - 1)
                if isinstance(b, int) and b == 0 and u == 1:
                    pe.wait_ge(s_flag, 1)
                qs = slice(t * P, (t + 1) * P)
                for r in range(2):
                    o = ps_s[:, u % 2, r, 0:BK]
                    cols = slice((g * HG + r * HB) * K, (g * HG + (r + 1) * HB) * K)
                    for c in range(DC):
                        mm(o, xn_hi[:, c, qs], t_hi[:, c, cols], start=c == 0, stop=False)
                        mm(o, xn_hi[:, c, qs], t_lo[:, c, cols], start=False, stop=False)
                        ins = mm(o, xn_lo[:, c, qs], t_hi[:, c, cols], start=False, stop=c == DC - 1)
                ins.then_inc(scores_done, 1)

            def transpose_probs(b, g, t):
                u = NT * g + t
                pe.wait_ge(probs_done, NU * b + u + 1)
                if isinstance(b, int) and b == 0 and u == 0:
                    for n in range(last_v - 2, last_v + 1):
                        evacuated(pe, n)
                for q in range(2):
                    m = 2 * t + q
                    if m < 2:
                        wait(pe, olo_done, NU * b + 2 * g + m - 1)
                    else:
                        pe.wait_ge(pt_copied, 8 * b + 4 * g + m - 1)
                    for h in range(HB):
                        hh = q * HB + h
                        ins = nc.tensor.transpose(ps_p[0:K, m % 2, h * P:(h + 1) * P],
                                                  probs[:, u, hh * K:(hh + 1) * K], ident[:])
                    ins.then_inc(pt_done, 1)

            def values(b, g):
                pe.wait_ge(pt_copied, 8 * b + 4 * g + 4)
                if g == 0:
                    pe.wait_ge(v_in, 16 * (b + 1))
                for i in range(2):
                    for pair in range(2):
                        for e in range(2):
                            h = 4 * i + 2 * pair + e
                            gh = g * HG + h
                            ins = mm(ps_p[e * DH:(e + 1) * DH, i, pair * Q:(pair + 1) * Q],
                                     v[:, gh * DH:(gh + 1) * DH], pt[:, h, :], start=True, stop=True)
                    ins.then_inc(pv_done, 1)

            def transpose_x(n):
                pe.wait_ge(xhat_done, NT * (n + 1))
                if isinstance(n, int) and n == 0:
                    evacuated(pe, last_t)
                claim(n - 1, "XT")
                for c in range(DC):
                    for t in range(NT):
                        ins = nc.tensor.transpose(ps_m[:, bank["XT"], c * Q + t * P:c * Q + (t + 1) * P],
                                                  x_hat[:, t, c * P:(c + 1) * P], ident[:])
                ins.then_inc(xt_done, 1)

            def transpose_x1(b):
                if last(b):
                    warm_up(0, WARM_UP[2])
                pe.wait_ge(x1hat_done, NT * b)
                for c in range(DC):
                    for t in range(NT):
                        ins = nc.tensor.transpose(ps_m[:, bank["X1T"], c * Q + t * P:c * Q + (t + 1) * P],
                                                  x1_hat[:, t, c * P:(c + 1) * P], ident[:])
                ins.then_inc(x2t_done, 1)
                if last(b):
                    warm_up(0, WARM_UP[3])

            def whole(ap, general):
                return ap.bitcast(F32) if general else ap

            def gate_up(b, f, general):
                if f == 0:
                    if isinstance(b, int) and b == 1:
                        pe.wait_ge(s_wf[0], 16)
                        pe.wait_ge(s_wf[1], 16)
                    pe.wait_ge(x2hi_done, b)
                    pe.wait_ge(x2lo_done, b)
                if not last(b):
                    claim(b, f"G{f}")
                fs = slice(f * P, (f + 1) * P)
                for w, at in ((wg, 0), (wu, Q)):
                    o = gate_up_psum(b, f)[:, at:at + Q]
                    for c in range(DC):
                        mm(o, whole(w[:, c, fs], general), whole(x2_hi[:, c, :], general), start=c == 0, stop=False)
                        ins = mm(o, whole(w[:, c, fs], general), whole(x2_lo[:, c, :], general), start=False, stop=c == DC - 1)
                ins.then_inc(gu_done, 1)

            def last_down(general):
                for f in range(FC):
                    pe.wait_ge(hlo_done, FC * (B - 1) + f + 1)
                    for t in range(NT):
                        o = ps_m[:, bank[f"D{t}"], 0:D]
                        ts = slice(t * P, (t + 1) * P)
                        mm(o, whole(h_hi[:, f, ts], general), whole(wd[:, f, :], general), start=f == 0, stop=False)
                        ins = mm(o, whole(h_lo[:, f, ts], general), whole(wd[:, f, :], general), start=False, stop=f == FC - 1)
                        if f == FC - 1:
                            ins.then_inc(down_done, 1)

            def down(b, t, general):
                if last(b):
                    if t == 0:
                        last_down(general)
                    return
                if t == 0:
                    if isinstance(b, int) and b == 1:
                        pe.wait_ge(s_wf[2], 16)
                    pe.wait_ge(hhi_done, FC * b)
                    pe.wait_ge(hlo_done, FC * b)
                claim(b, f"D{t}")
                o = ps_m[:, bank[f"D{t}"], 0:D]
                ts = slice(t * P, (t + 1) * P)
                for f in range(FC):
                    mm(o, whole(h_hi[:, f, ts], general), whole(wd[:, f, :], general), start=f == 0, stop=False)
                    ins = mm(o, whole(h_lo[:, f, ts], general), whole(wd[:, f, :], general), start=False, stop=f == FC - 1)
                ins.then_inc(down_done, 1)

            def project(b, t):
                if isinstance(b, int) and b == 0 and t == 0:
                    pe.wait_ge(s_wol, 1)
                if t == 0:
                    pe.wait_ge(ohi_done, NU * (b + 1))
                    pe.wait_ge(olo_done, NU * (b + 1))
                claim(b, f"O{t}")
                o = ps_m[:, bank[f"O{t}"], 0:D]
                ts = slice(t * P, (t + 1) * P)
                for i in range(IC):
                    mm(o, o_hi[:, i, ts], wo_hi[:, i, :], start=i == 0, stop=False)
                    mm(o, o_hi[:, i, ts], wo_lo[:, i, :], start=False, stop=False)
                    ins = mm(o, o_lo[:, i, ts], wo_hi[:, i, :], start=False, stop=i == IC - 1)
                ins.then_inc(proj_done, 1)

            def stages_of(general):
                stages = {"X1T": ("ffn", transpose_x1), "XT": ("next", transpose_x)}
                for u in range(NU):
                    stages[f"S{u}"] = ("next" if u < HOISTED else "now", scores, u)
                    stages[f"T{u}"] = ("now", transpose_probs, u // NT, u % NT)
                for t in range(NT):
                    stages[f"V{t}"] = ("now", values, t)
                    stages[f"D{t}"] = ("ffn", down, t, general)
                    stages[f"O{t}"] = ("now", project, t)
                for f in range(FC):
                    stages[f"G{f}"] = ("ffn", gate_up, f, general)
                stages["job"], stages["fill"] = job, lambda name: job(stand_in[name])
                stages["FL"] = ("start", transpose_largest)
                return stages

            start(PE_START, stages_of(False))
            pe.wait_ge(s_flag, 2)
            inexact_here = pe.value_load(inexact[0:1, 0:1])
            with pe.If(inexact_here > 0):
                batches(pe, PE_ORDER, stages_of(True))
            with pe.Else():
                batches(pe, PE_ORDER, stages_of(False))

        @block.scalar
        def _(act):
            act.dma_start(gamma[:], ln_gamma.rearrange("(c p) -> p c", p=P),
                          allow_slow_non_contiguous=True).then_inc(s_in["small"], 16)
            act.dma_start(beta[:], ln_beta.rearrange("(c p) -> p c", p=P),
                          allow_slow_non_contiguous=True).then_inc(s_in["small"], 16)
            act.dma_start(tgate[:], gate.rearrange("(a n) -> a n", a=1).to_broadcast([P, 1])).then_inc(s_in["small"], 16)
            act.dma_start(bias[:], b_out.rearrange("(a n) -> a n", a=1).to_broadcast([P, D])).then_inc(s_in["small"], 16)

            def copy(n):
                act.wait_ge(s_job, n + 1)
                if n < first_t:
                    for part in parts(n):
                        ins = nc.scalar.copy(part[1], part[0])
                    ins.then_inc(s_act, 1)
                else:
                    if jobs[n][0] == "v" and jobs[n][1] == VS:
                        act.wait_ge(s_vfirst, 16)
                    nc.scalar.copy(target(n), psum_of(n)).then_inc(s_act, 1)

            def wk_part(i):
                cols = slice(i * INNER // WP, (i + 1) * INNER // WP)
                act.wait_ge(s_wk[i], 16)
                nc.scalar.copy(wk_hi[:, :, cols], wk_raw[:, :, cols]).then_inc(s_wkh, 1)

            def wout_hi():
                act.wait_ge(s_in["wo"], 16)
                act.wait_ge(s_job, last_v + 1)
                nc.scalar.copy(wo_hi[:], wo_raw[:]).then_inc(s_woh, 1)

            for n in act_jobs:
                if n < first_v:
                    copy(n)
                if jobs[n] == ("ctx", RC - 1):
                    for i in range(WP // 2):
                        wk_part(i)
                if jobs[n][0] == "k" and jobs[n][1] < WP // 2:
                    wk_part(jobs[n][1] + WP // 2)
                if n == first_t - 1:
                    act.wait_ge(s_in["small"], 64)
                    nc.scalar.activation(tgate[:], tgate[:], ACT.Tanh).then_inc(s_tgate, 1)

            def exponentials(b, u):
                act.wait_ge(sub_done, NU * b + u + 1)
                nc.scalar.activation(probs[:, u, :], probs[:, u, :], ACT.Exp, scale=SCALE).then_inc(exp_done, 1)

            def copy_pt(b, g, t):
                for q in range(2):
                    m = 4 * g + 2 * t + q
                    act.wait_ge(pt_done, 8 * b + m + 1)
                    if t == 0 and q == 0:
                        wait(act, pv_done, NU * b + 2 * g)
                        if isinstance(b, int) and b == 0 and g == 0:
                            act.wait_ge(s_vrest, 16 * (RC - 1))
                    nc.scalar.copy(pt[:, q * HB:(q + 1) * HB, t * P:(t + 1) * P],
                                   ps_p[0:K, m % 2, :].rearrange("k (h q) -> k h q", h=HB)).then_inc(pt_copied, 1)

            def copy_o(b, g):
                for i in range(2):
                    n = 2 * g + i
                    act.wait_ge(pv_done, NU * b + n + 1)
                    if n == 0:
                        wait(act, proj_done, NT * b)
                    nc.scalar.copy(o_hi[:, 2 * n:2 * n + 2, :],
                                   ps_p[:, i, :].rearrange("p (i q) -> p i q", i=2)).then_inc(ohi_done, 1)

            def split_t(n, g):
                if isinstance(n, int) and n == 0:
                    act.wait_ge(s_job, last_t + 1)
                    act.wait_ge(s_dve, max(by_dve[m] for m in by_dve if m <= last_t))
                    act.wait_ge(s_act, max(by_act[m] for m in by_act if m <= last_t))
                if not (isinstance(n, int) and n == 0):
                    act.wait_ge(scores_done, NU * (n - 1) + NT * (g + 1))
                    act.wait_ge(tlo_done, 2 * (n - 1) + g + 1)
                nc.scalar.copy(t_hi[:, :, g * GK:(g + 1) * GK],
                               t_all[:, :, n, g * GK:(g + 1) * GK]).then_inc(thi_done, 1)

            def affine_x(n):
                act.wait_ge(xt_done, n + 1)
                if not (isinstance(n, int) and n == 0):
                    act.wait_ge(xnhi_done, n)
                    act.wait_ge(xnlo_done, n)
                for c in range(DC):
                    nc.scalar.activation(xn[:, c, :], ps_m[:, bank["XT"], c * Q:(c + 1) * Q], ACT.Identity,
                                         scale=gamma[:, c:c + 1], bias=beta[:, c:c + 1]).then_inc(xn_done, 1)
                act.wait_ge(xn_done, DC * (n + 1))
                if not (isinstance(n, int) and n == 0):
                    act.wait_ge(scores_done, NU * n)
                nc.scalar.copy(xn_hi[:], xn[:]).then_inc(xnhi_done, 1)

            def split_x2(b):
                act.wait_ge(x2t_done, b)
                nc.scalar.copy(x2_hi[:], ps_m[:, bank["X1T"], :].rearrange("p (c q) -> p c q", c=DC)).then_inc(x2hi_done, 1)

            def tanh(b, f):
                act.wait_ge(gu_done, FC * (b - 1) + f + 1)
                if f >= 2:
                    act.wait_ge(gated, FC * (b - 1) + f - 1)
                nc.scalar.activation(tanh_g[:, f % 2, :], gate_up_psum(b, f)[:, 0:Q], ACT.Tanh,
                                     scale=QUANT / 2).then_inc(tanh_done, 1)

            def split_h(b, f):
                act.wait_ge(hid_done, FC * (b - 1) + f + 1)
                nc.scalar.copy(h_hi[:, f, :], hid[:, f % 2, :]).then_inc(hhi_done, 1)

            stages = {"X1": ("ffn", split_x2), "X": ("next", affine_x),
                      "Ta": ("next", split_t, 0), "Tb": ("next", split_t, 1)}
            for u in range(NU):
                stages[f"E{u}"] = ("next" if u < HOISTED else "now", exponentials, u)
                stages[f"C{u}"] = ("now", copy_pt, u // NT, u % NT)
            for g in range(2):
                stages[f"O{g}"] = ("now", copy_o, g)
            for f in range(FC):
                stages[f"t{f}"] = ("ffn", tanh, f)
                stages[f"h{f}"] = ("ffn", split_h, f)
            stages["job"], stages["WO"] = copy, ("start", wout_hi)
            start(ACT_START, stages)
            batches(act, ACT_ORDER, stages)

        @block.gpsimd
        def _(pool):
            nc.gpsimd.memset(ident[:], 0.0).then_inc(s_ident0, 1)
            pool.wait_ge(s_ident0, 1)
            nc.gpsimd.affine_select(out=ident[:], in_=ident[:], compare_op=ALU.not_equal, fill=1.0,
                                    base=0, pattern=[[-1, P]], channel_multiplier=1).then_inc(s_ident, 1)
            for i, value in enumerate((EPS, -0.5, 1.5)):
                nc.gpsimd.memset(consts[:, i, :], value).then_inc(consts_set, 1)
            for i in range(WP):
                cols = slice(i * INNER // WP, (i + 1) * INNER // WP)
                pool.wait_ge(s_wkh, i + 1)
                nc.gpsimd.tensor_tensor(wk_lo[:, :, cols], wk_raw[:, :, cols], wk_hi[:, :, cols].bitcast(F32),
                                        ALU.subtract).then_inc(s_wkl, 1)
            pool.wait_ge(s_in["wv"], 16)
            nc.gpsimd.tensor_copy(wv_hi, wv_raw[:]).then_inc(s_wvh, 1)
            pool.wait_ge(s_wvh, 1)
            nc.gpsimd.tensor_tensor(wv_lo, wv_raw[:], wv_hi.bitcast(F32), ALU.subtract).then_inc(s_wvl, 1)
            steps = [0]

            def step(ins):
                steps[0] += 1
                ins.then_inc(s_ln, 1)
                if steps[0] < X_STEPS:
                    pool.wait_ge(s_ln, steps[0])

            def nothing():
                pass

            def x_scales():
                pool.wait_ge(consts_set, 3)
                pool.wait_ge(s_aggr, B * NT)
                tt = nc.gpsimd.tensor_tensor
                step(nc.gpsimd.tensor_copy(mean1[:], mv1[:, :, 0]))
                step(nc.gpsimd.tensor_scalar(var1[:], mv1[:, :, 1], 1.0 + EPS, EPS * EPS, ALU.mult, ALU.add))
                rsqrt(step, nothing, rstd1[:], var1[:], half1[:], tmp1[:])
                assert steps[0] == X_STEPS

            def wout_lo():
                pool.wait_ge(s_woh, 1)
                nc.gpsimd.tensor_tensor(wo_lo[:], wo_raw[:], wo_hi[:].bitcast(F32), ALU.subtract).then_inc(s_wol, 1)

            def normalise(b, u):
                pool.wait_ge(rec_done, NU * b + u + 1)
                p = probs[:, u, :].rearrange("p (h k) -> p h k", k=K)
                nc.gpsimd.tensor_tensor(p, p, total[:, u, :].unsqueeze(2).to_broadcast([P, HG, K]),
                                        ALU.mult).then_inc(probs_done, 1)

            def split_t(n, g):
                pool.wait_ge(thi_done, 2 * n + g + 1)
                cols = slice(g * GK, (g + 1) * GK)
                nc.gpsimd.tensor_tensor(t_lo[:, :, cols], t_all[:, :, n, cols], t_hi[:, :, cols].bitcast(F32),
                                        ALU.subtract).then_inc(tlo_done, 1)

            def split_xn(n):
                pool.wait_ge(xnhi_done, n + 1)
                nc.gpsimd.tensor_tensor(xn_lo[:], xn[:], xn_hi[:].bitcast(F32), ALU.subtract).then_inc(xnlo_done, 1)

            def split_h(b, f):
                pool.wait_ge(hhi_done, FC * (b - 1) + f + 1)
                nc.gpsimd.tensor_tensor(h_lo[:, f, :], hid[:, f % 2, :], h_hi[:, f, :].bitcast(F32),
                                        ALU.subtract).then_inc(hlo_done, 1)

            def norm_scale(b):
                if isinstance(b, int) and b == B - 1:
                    return
                done = [0]
                pool.wait_ge(aggr_done, NT * (b + 1))

                def step(ins):
                    done[0] += 1
                    ins.then_inc(ln_step, 1)
                    if done[0] < LN_STEPS:
                        pool.wait_ge(ln_step, LN_STEPS * b + done[0])

                def carry():
                    nc.gpsimd.tensor_tensor(spare_pool[:], consts[:, 0, 0:NT], consts[:, 1, 0:NT], ALU.mult)

                step(nc.gpsimd.tensor_tensor(var_eps[:], mv[:, :, 1], consts[:, 0, 0:NT], ALU.add))
                rsqrt(step, carry, rstd[:], var_eps[:], half_var[:], tmp[:])
                assert done[0] == LN_STEPS

            def bias_x(b):
                if isinstance(b, int) and b == 0:
                    pool.wait_ge(s_bias, 1)
                pool.wait_ge(xres_in, 16 * (b + 1))
                nc.gpsimd.tensor_tensor(residual_of(b), residual_of(b), bias[:].unsqueeze(1).to_broadcast([P, NT, D]),
                                        ALU.add).then_inc(xres_biased, 1)

            stages = {"Ta": ("next", split_t, 0), "Tb": ("next", split_t, 1), "B": ("now", bias_x),
                      "X": ("next", split_xn), "LN": ("now", norm_scale)}
            for u in range(NU):
                stages[f"P{u}"] = ("next" if u < HOISTED else "now", normalise, u)
            for f in range(FC):
                stages[f"h{f}"] = ("ffn", split_h, f)
            stages["XS"], stages["WO"] = ("start", x_scales), ("start", wout_lo)
            start(POOL_START, stages)
            batches(pool, POOL_ORDER, stages)

        @block.vector
        def _(dve):
            def copy(n):
                dve.wait_ge(s_job, n + 1)
                if n < first_t:
                    dve.wait_ge(s_act, by_act[n])
                    for psum, hi, lo in parts(n):
                        ins = nc.vector.tensor_tensor(lo, psum, hi.bitcast(F32), ALU.subtract)
                    ins.then_inc(s_dve, 1)
                else:
                    if jobs[n][0] == "v" and jobs[n][1] == VS:
                        dve.wait_ge(s_vfirst, 16)
                    nc.vector.tensor_copy(target(n), psum_of(n)).then_inc(s_dve, 1)

            def stat(i):
                b, t = B - 1 - i // NT, i % NT
                if b == 0:
                    dve.wait_ge(xln_in, 16)
                else:
                    dve.wait_ge(s_xs[b % 2], 16 * ((B - b - 1) // 2 + 1))
                if i >= 2:
                    dve.wait_ge(s_aggr, i - 1)
                nc.vector.bn_stats(stats1[:, i % 2, :], (x_hat if b % 2 else x_ln)[:, t, :]).then_inc(s_stat, 1)
                dve.wait_ge(s_stat, i + 1)
                nc.vector.bn_aggr(mv1[:, NT * b + t, :], stats1[:, i % 2, :]).then_inc(s_aggr, 1)

            def to_float(i):
                name, raw = (("wg", wg_raw), ("wu", wu_raw), ("wd", wd_raw))[i]
                dve.wait_ge(s_in[name], 16)
                nc.vector.tensor_copy(raw[:], raw[:].bitcast(I32)).then_inc(s_float[i], 1)

            def largest_weight(i):
                dve.wait_ge(s_float[i], 1)
                raw = (wg_raw, wu_raw, wd_raw)[i]
                nc.vector.tensor_reduce(largest[:, i:i + 1], raw[:].rearrange("p a b -> p (a b)"), AXIS_X, ALU.max,
                                        apply_absolute_value=True).then_inc(s_large[i], 1)

            def largest_of_partition():
                for s in s_large:
                    dve.wait_ge(s, 1)
                nc.vector.reduce_max(largest_row[:], largest[:], AXIS_X).then_inc(s_row, 1)

            def exactness():
                dve.wait_ge(s_rows, 1)
                nc.vector.reduce_max(largest_of_all[:], ps[0:1, 3, 0:P], AXIS_X).then_inc(s_flag, 1)
                dve.wait_ge(s_flag, 1)
                nc.vector.tensor_scalar(inexact[:], largest_of_all[:], EXACT, None, ALU.is_gt).then_inc(s_flag, 1)

            stats_at = 0
            for n in dve_jobs:
                if n < first_v:
                    copy(n)
                if first_t <= n < first_v:
                    for _ in range(STATS_PER_JOB):
                        if stats_at < B * NT:
                            stat(stats_at)
                            stats_at += 1
                if n == first_t - 1:
                    dve.wait_ge(s_tgate, 1)
                    nc.vector.tensor_scalar(bias[:], bias[:], tgate[:, 0:1], None, ALU.mult).then_inc(s_bias, 1)

            def maxima(b, u):
                dve.wait_ge(scores_done, NU * b + u + 1)
                s = ps_s[:, u % 2, :, 0:BK].rearrange("p r (h k) -> p r h k", k=K)
                if not (isinstance(b, int) and b == 0):
                    dve.wait_ge(sub_done, NU * (b - 1) + u + 1)
                nc.vector.reduce_max(top[:, u, :].rearrange("p (r h) -> p r h", r=2), s, AXIS_X).then_inc(max_done, 1)
                dve.wait_ge(max_done, NU * b + u + 1)
                if not (isinstance(b, int) and b == 0):
                    dve.wait_ge(pt_done, 8 * (b - 1) + 2 * (u + 1))
                nc.vector.tensor_tensor(
                    probs[:, u, :].rearrange("p (r h k) -> p r h k", r=2, k=K), s,
                    top[:, u, :].rearrange("p (r h) -> p r h", r=2).unsqueeze(3).to_broadcast([P, 2, HB, K]),
                    ALU.subtract).then_inc(sub_done, 1)

            def sums(b, u):
                dve.wait_ge(exp_done, NU * b + u + 1)
                if not (isinstance(b, int) and b == 0):
                    dve.wait_ge(probs_done, NU * (b - 1) + u + 1)
                nc.vector.reduce_sum(total[:, u, :], probs[:, u, :].rearrange("p (h k) -> p h k", k=K),
                                     AXIS_X).then_inc(sum_done, 1)
                dve.wait_ge(sum_done, NU * b + u + 1)
                nc.vector.reciprocal(total[:, u, :], total[:, u, :]).then_inc(rec_done, 1)

            def split_o(b, g):
                for i in range(2):
                    n = 2 * g + i
                    dve.wait_ge(ohi_done, NU * b + n + 1)
                    if n == 0:
                        wait(dve, proj_done, NT * b)
                        if isinstance(b, int) and b == 0:
                            dve.wait_ge(s_wol, 1)
                    nc.vector.tensor_tensor(o_lo[:, 2 * n:2 * n + 2, :],
                                            ps_p[:, i, :].rearrange("p (i q) -> p i q", i=2),
                                            o_hi[:, 2 * n:2 * n + 2, :].bitcast(F32), ALU.subtract).then_inc(olo_done, 1)

            def split_x2(b):
                dve.wait_ge(x2hi_done, b)
                nc.vector.tensor_tensor(x2_lo[:], ps_m[:, bank["X1T"], :].rearrange("p (c q) -> p c q", c=DC),
                                        x2_hi[:].bitcast(F32), ALU.subtract).then_inc(x2lo_done, 1)

            def hidden(b, f):
                n = FC * (b - 1) + f
                dve.wait_ge(tanh_done, n + 1)
                if f >= 2:
                    dve.wait_ge(hlo_done, n - 1)
                nc.vector.scalar_tensor_tensor(hid[:, f % 2, :], tanh_g[:, f % 2, :], 1.0,
                                               gate_up_psum(b, f)[:, 0:Q], ALU.add, ALU.mult).then_inc(gated, 1)
                dve.wait_ge(gated, n + 1)
                nc.vector.tensor_tensor(hid[:, f % 2, :], hid[:, f % 2, :], gate_up_psum(b, f)[:, Q:2 * Q],
                                        ALU.mult).then_inc(hid_done, 1)

            def normalise_x(n):
                if isinstance(n, int) and n == 0:
                    dve.wait_ge(s_ln, X_STEPS)
                dve.wait_ge(xln_in, 16 * (n + 1))
                if not (isinstance(n, int) and n == 0):
                    dve.wait_ge(xt_done, n)
                for t in range(NT):
                    col = NT * n + t
                    at = slice(col, col + 1) if isinstance(n, int) else bass.ds(col, 1)
                    nc.vector.tensor_scalar(x_hat[:, t, :], x_ln[:, t, :], mean1[:, at], rstd1[:, at],
                                            ALU.subtract, ALU.mult).then_inc(xhat_done, 1)

            def result(b, t):
                dve.wait_ge(down_done, NT * (b - 1) + t + 1)
                x1 = residual_of(b, 1)[:, t, :]
                nc.vector.scalar_tensor_tensor(x1, ps_m[:, bank[f"D{t}"], 0:D], 0.5 * QUANT ** 3, x1, ALU.mult, ALU.add).then_inc(y_done, 1)

            def residual(b, t):
                dve.wait_ge(proj_done, NT * b + t + 1)
                if t == 0:
                    dve.wait_ge(xres_biased, b + 1)
                x1 = residual_of(b)[:, t, :]
                nc.vector.scalar_tensor_tensor(x1, ps_m[:, bank[f"O{t}"], 0:D], tgate[:, 0:1], x1,
                                               ALU.mult, ALU.add).then_inc(x1_done, 1)
                dve.wait_ge(x1_done, NT * b + t + 1)
                nc.vector.bn_stats(stats[:, t, :], x1).then_inc(stat_done, 1)

            def aggregate(b):
                dve.wait_ge(stat_done, NT * (b + 1))
                nc.vector.memset(spare[:], 0.0).then_inc(spare_cleared, 1)
                for t in range(NT):
                    nc.vector.bn_aggr(mv[:, t, :], stats[:, t, :]).then_inc(aggr_done, 1)
                if isinstance(b, int) and b == B - 1:
                    last_norm_scale()

            def last_norm_scale():
                dve.wait_ge(aggr_done, NT * B)
                done = [LN_STEPS * (B - 1)]

                def step(ins, signals=1):
                    done[0] += signals
                    ins.then_inc(ln_step, signals)
                    if done[0] < LN_STEPS * B:
                        dve.wait_ge(ln_step, done[0])

                step(nc.vector.tensor_scalar(var_eps[:], mv[:, :, 1], EPS, None, ALU.add))
                step(nc.vector.tensor_scalar(rstd[:].bitcast(I32), var_eps[:].bitcast(I32), -0.5, RSQRT_SEED,
                                             ALU.mult, ALU.add))
                for i in range(3):
                    step(nc.vector.tensor_tensor(tmp[:], rstd[:], rstd[:], ALU.mult))
                    step(nc.vector.scalar_tensor_tensor(tmp[:], tmp[:], -0.5, var_eps[:], ALU.mult, ALU.mult))
                    step(nc.vector.scalar_tensor_tensor(rstd[:], tmp[:], 1.5, rstd[:], ALU.add, ALU.mult),
                         LN_STEPS - 10 if i == 2 else 1)

            def normalise_x1(b):
                dve.wait_ge(ln_step, LN_STEPS * (b + 1))
                for t in range(NT):
                    nc.vector.tensor_scalar(x1_hat[:, t, :], residual_of(b, 1)[:, t, :], mv[:, t, 0:1], rstd[:, t:t + 1],
                                            ALU.subtract, ALU.mult).then_inc(x1hat_done, 1)

            stages = {"X1": ("ffn", split_x2), "LN": ("next", normalise_x), "AG": ("now", aggregate),
                      "LN1": ("ffn", lambda b: normalise_x1(b - 1))}
            for u in range(NU):
                stages[f"M{u}"] = ("next" if u < HOISTED else "now", maxima, u)
                stages[f"Z{u}"] = ("next" if u < HOISTED else "now", sums, u)
            for t in range(NT):
                stages[f"O{t}"] = ("now", split_o, t)
                stages[f"Y{t}"] = ("ffn", result, t)
                stages[f"R{t}"] = ("now", residual, t)
            for f in range(FC):
                stages[f"H{f}"] = ("ffn", hidden, f)
            for i in range(3):
                stages[f"F{i}"] = ("start", to_float, i)
            stages["job"] = copy
            for i in range(3):
                stages[f"B{i}"] = ("start", largest_weight, i)
            stages["BC"], stages["BR"] = ("start", largest_of_partition), ("start", exactness)
            stages["fill"] = lambda name: copy(copied_at[name]) if name in copied_at else None
            start(DVE_START, stages)
            batches(dve, DVE_ORDER, stages)


_INS = ["x", "ctx_1024", "L0_xattn_ln_gamma", "L0_xattn_ln_beta", "L0_xattn_w_q", "L0_xattn_w_kv",
        "L0_xattn_w_out", "L0_xattn_b_out", "L0_xattn_gate", "L0_ffn_w_gate", "L0_ffn_w_up", "L0_ffn_w_down"]


def kernel(**inputs):
    import numpy as np
    import concourse.bacc as bacc
    from concourse.bass_utils import run_bass_kernel_spmd

    nc = bacc.Bacc("TRN2", target_bir_lowering=False, num_devices=1)
    arrays, args = {}, []
    for name in _INS:
        a = np.ascontiguousarray(inputs[name])
        arrays[f"in_{name}"] = a
        args.append(nc.dram_tensor(f"in_{name}", a.shape, mybir.dt.from_np(a.dtype), kind="ExternalInput").ap())
    shape = arrays["in_x"].shape
    args.append(nc.dram_tensor("out", shape, F32, kind="ExternalOutput").ap())
    xattn_ffn_kernel(nc, *args)
    r = run_bass_kernel_spmd(nc, [arrays], core_ids=[0])
    return r.results[0]["out"]
```
